# Optimizing a Trainium2 kernel written in Bass

```python
import numpy as np
import jax
import jax.numpy as jnp

def _softmax(x, axis=-1):
    return jax.nn.softmax(x, axis=axis)

def _gelu(x):
    return jax.nn.gelu(x, approximate=True)

def _silu(x):
    return jax.nn.silu(x)

def _sigmoid(x):
    return jax.nn.sigmoid(x)

def _layernorm(x, axis=-1, eps=1e-05):
    m = jnp.mean(x, axis=axis, keepdims=True)
    v = jnp.var(x, axis=axis, keepdims=True)
    return (x - m) / jnp.sqrt(v + eps)

def _scatter_add(tgt, idx, src, axis=0):
    return tgt.at[idx].add(src)

def _segment_sum(src, seg, n):
    return jax.ops.segment_sum(src, seg, n)
kernel_name = 'mk_gnn_ffn_d1_gnn_r32_d41fe6'

def setup_inputs(seed: int=0):
    np.random.seed(seed)
    _w = jnp.asarray

    def _rec_inputs():
        import jax
        import jax.numpy as jnp
        _gk = jax.random.key(seed)
        x = -0.0005963 + 1.001 * jax.random.normal(jax.random.fold_in(_gk, 1), (96, 1024), jnp.float32)
        src = jax.random.randint(jax.random.fold_in(_gk, 2), (1536,), 0, 96, jnp.int32)
        dst = jnp.minimum((96 * jax.random.uniform(jax.random.fold_in(_gk, 3), (1536,)) ** 2.0).astype(jnp.int32), 3071)
        _o = jnp.argsort(dst, stable=True)
        src = src[_o]
        dst = dst[_o]
        edge_type_5 = jax.random.randint(jax.random.fold_in(_gk, 12), (1536,), 0, 5, jnp.int32)
        return (x, src, dst, edge_type_5)
    x, src, dst, edge_type_5 = _rec_inputs()

    def _L0_gnn_setup():
        import jax, jax.numpy as jnp
        import numpy as np
        N = 96
        E = 3072
        IN_F = 1024
        OUT_F = 1024
        H = 16
        D = OUT_F // H
        NUM_ETYPES = 4

        def _build_mask(edge_index, edge_type, edge_type_weights, dtype):
            src, dst = (edge_index[0], edge_index[1])
            w = jax.nn.softplus(edge_type_weights)
            mask = jnp.full((N, N), -jnp.inf, dtype=dtype)
            mask = mask.at[src, dst].set(w[edge_type - 1])
            diag = jnp.diagonal(mask)
            idx = jnp.arange(N)
            mask = mask.at[idx, idx].set(jnp.where(jnp.isneginf(diag), w[3], diag))
            return mask
        key = jax.random.key(seed)
        ks = jax.random.split(key, 20)
        p = lambda k, shape: jax.random.normal(k, shape, dtype=jnp.float32) * 0.02
        return {'x': jax.random.normal(ks[0], (N, IN_F), dtype=jnp.float32), 'edge_index': jax.random.randint(ks[1], (2, E), 0, N), 'edge_type': jax.random.randint(ks[2], (E,), 1, NUM_ETYPES + 1), 'edge_type_weights': jnp.ones((NUM_ETYPES,), jnp.float32) + 0.1 * jax.random.normal(ks[3], (NUM_ETYPES,), dtype=jnp.float32), 'wq': p(ks[4], (OUT_F, IN_F)), 'bq': p(ks[5], (OUT_F,)), 'wk': p(ks[6], (OUT_F, IN_F)), 'bk': p(ks[7], (OUT_F,)), 'wv': p(ks[8], (OUT_F, IN_F)), 'bv': p(ks[9], (OUT_F,)), 'wiq': p(ks[10], (OUT_F, OUT_F)), 'biq': p(ks[11], (OUT_F,)), 'wik': p(ks[12], (OUT_F, OUT_F)), 'bik': p(ks[13], (OUT_F,)), 'wiv': p(ks[14], (OUT_F, OUT_F)), 'biv': p(ks[15], (OUT_F,)), 'wo': p(ks[16], (OUT_F, OUT_F)), 'bo': p(ks[17], (OUT_F,))}
    _L0_gnn_all = _L0_gnn_setup()
    _L0_gnn_in = {k: v for k, v in _L0_gnn_all.items() if k in ('edge_type_weights', 'wq', 'bq', 'wk', 'bk', 'wv', 'bv', 'wiq', 'biq', 'wik', 'bik', 'wiv', 'biv', 'wo', 'bo')}
    del _L0_gnn_all

    def _L0_ffn_setup():
        import jax, jax.numpy as jnp
        import numpy as np
        from jax import lax
        D = 1024
        H = 128
        E = 8
        TOPK = 2
        key = jax.random.key(seed)
        ks = jax.random.split(key, 7)
        s = 0.02
        return {'x': jax.random.normal(ks[0], (2, 64, D), dtype=jnp.float32), 'W1': jax.random.normal(ks[1], (E, D, H), dtype=jnp.float32) * s, 'b1': jnp.zeros((E, H), dtype=jnp.float32), 'W2': jax.random.normal(ks[2], (E, H, D), dtype=jnp.float32) * s, 'b2': jnp.zeros((E, D), dtype=jnp.float32), 'Wr': jax.random.normal(ks[3], (D, E), dtype=jnp.float32) * s, 'br': jnp.zeros((E,), dtype=jnp.float32)}
    _L0_ffn_all = _L0_ffn_setup()
    _L0_ffn_in = {k: v for k, v in _L0_ffn_all.items() if k in ('W1', 'b1', 'W2', 'b2', 'Wr', 'br')}
    del _L0_ffn_all
    return {'x': x, 'src': src, 'dst': dst, 'edge_type_5': edge_type_5, 'L0_gnn_edge_type_weights': _L0_gnn_in['edge_type_weights'], 'L0_gnn_wq': _L0_gnn_in['wq'], 'L0_gnn_bq': _L0_gnn_in['bq'], 'L0_gnn_wk': _L0_gnn_in['wk'], 'L0_gnn_bk': _L0_gnn_in['bk'], 'L0_gnn_wv': _L0_gnn_in['wv'], 'L0_gnn_bv': _L0_gnn_in['bv'], 'L0_gnn_wiq': _L0_gnn_in['wiq'], 'L0_gnn_biq': _L0_gnn_in['biq'], 'L0_gnn_wik': _L0_gnn_in['wik'], 'L0_gnn_bik': _L0_gnn_in['bik'], 'L0_gnn_wiv': _L0_gnn_in['wiv'], 'L0_gnn_biv': _L0_gnn_in['biv'], 'L0_gnn_wo': _L0_gnn_in['wo'], 'L0_gnn_bo': _L0_gnn_in['bo'], 'L0_ffn_W1': _L0_ffn_in['W1'], 'L0_ffn_b1': _L0_ffn_in['b1'], 'L0_ffn_W2': _L0_ffn_in['W2'], 'L0_ffn_b2': _L0_ffn_in['b2'], 'L0_ffn_Wr': _L0_ffn_in['Wr'], 'L0_ffn_br': _L0_ffn_in['br']}

def reference(x, src, dst, edge_type_5, L0_gnn_edge_type_weights, L0_gnn_wq, L0_gnn_bq, L0_gnn_wk, L0_gnn_bk, L0_gnn_wv, L0_gnn_bv, L0_gnn_wiq, L0_gnn_biq, L0_gnn_wik, L0_gnn_bik, L0_gnn_wiv, L0_gnn_biv, L0_gnn_wo, L0_gnn_bo, L0_ffn_W1, L0_ffn_b1, L0_ffn_W2, L0_ffn_b2, L0_ffn_Wr, L0_ffn_br):
    import jax
    import jax.numpy as jnp

    def _L0_gnn_ref(x, edge_index, edge_type, edge_type_weights, wq, bq, wk, bk, wv, bv, wiq, biq, wik, bik, wiv, biv, wo, bo):
        import jax, jax.numpy as jnp
        import numpy as np
        N = 96
        E = 3072
        IN_F = 1024
        OUT_F = 1024
        H = 16
        D = OUT_F // H
        NUM_ETYPES = 4

        def _build_mask(edge_index, edge_type, edge_type_weights, dtype):
            src, dst = (edge_index[0], edge_index[1])
            w = jax.nn.softplus(edge_type_weights)
            mask = jnp.full((N, N), -jnp.inf, dtype=dtype)
            mask = mask.at[src, dst].set(w[edge_type - 1])
            diag = jnp.diagonal(mask)
            idx = jnp.arange(N)
            mask = mask.at[idx, idx].set(jnp.where(jnp.isneginf(diag), w[3], diag))
            return mask
        q = x @ wq.T + bq
        k = x @ wk.T + bk
        v = x @ wv.T + bv
        q2 = (q @ wiq.T + biq).reshape(N, H, D).transpose(1, 0, 2)
        k2 = (k @ wik.T + bik).reshape(N, H, D).transpose(1, 0, 2)
        v2 = (v @ wiv.T + biv).reshape(N, H, D).transpose(1, 0, 2)
        mask = _build_mask(edge_index, edge_type, edge_type_weights, x.dtype)
        scale = 1.0 / np.sqrt(D).astype(np.float32)
        scores = jnp.einsum('hnd,hmd->hnm', q2, k2) * scale + mask[None]
        attn = jax.nn.softmax(scores, axis=-1)
        out = jnp.einsum('hnm,hmd->hnd', attn, v2)
        out = out.transpose(1, 0, 2).reshape(N, OUT_F)
        return out @ wo.T + bo

    def _L0_ffn_ref(x, W1, b1, W2, b2, Wr, br):
        import jax, jax.numpy as jnp
        import numpy as np
        from jax import lax
        D = 1024
        H = 128
        E = 8
        TOPK = 2
        B, S, _ = x.shape
        xf = x.reshape(-1, D)
        logits = xf @ Wr + br
        topv, _ = lax.top_k(logits, TOPK)
        thresh = topv[:, TOPK - 1:TOPK]
        masked = jnp.where(logits >= thresh, logits, -jnp.inf)
        weights = jax.nn.softmax(masked, axis=-1)
        h = jax.nn.gelu(jnp.einsum('td,edh->eth', xf, W1) + b1[:, None, :], approximate=False)
        expert_out = jnp.einsum('eth,ehd->etd', h, W2) + b2[:, None, :]
        out = jnp.einsum('etd,te->td', expert_out, weights)
        return out.reshape(B, S, D)
    edge_index = jnp.stack([src, dst])
    x = x + _L0_gnn_ref(_layernorm(x, axis=-1), edge_index, edge_type_5, L0_gnn_edge_type_weights, L0_gnn_wq, L0_gnn_bq, L0_gnn_wk, L0_gnn_bk, L0_gnn_wv, L0_gnn_bv, L0_gnn_wiq, L0_gnn_biq, L0_gnn_wik, L0_gnn_bik, L0_gnn_wiv, L0_gnn_biv, L0_gnn_wo, L0_gnn_bo)
    x = x + _L0_ffn_ref(_layernorm(x, axis=-1)[None], L0_ffn_W1, L0_ffn_b1, L0_ffn_W2, L0_ffn_b2, L0_ffn_Wr, L0_ffn_br)[0]
    return x

_drawn_inputs = setup_inputs


def setup_inputs(seed=0):
    import zlib

    import numpy as np

    out = dict(_drawn_inputs(seed))
    spreads = {'L0_ffn_b1': (0.0, 0.776), 'L0_ffn_b2': (0.0, 0.1), 'L0_ffn_br': (0.0, 0.1)}
    factors = {'L0_gnn_edge_type_weights': 6.846,
     'L0_gnn_wq': 3.931,
     'L0_gnn_bq': 8.0,
     'L0_gnn_wk': 3.886,
     'L0_gnn_bk': 8.0,
     'L0_gnn_bv': 6.284,
     'L0_gnn_wiq': 4.098,
     'L0_gnn_biq': 8.0,
     'L0_gnn_wik': 3.725,
     'L0_gnn_bik': 8.0,
     'L0_gnn_biv': 3.635}
    for name, (base, spread) in spreads.items():
        noise = np.random.default_rng([zlib.crc32(name.encode()), seed]).standard_normal(out[name].shape)
        drawn = base * np.exp(spread * noise) if base else spread * noise
        out[name] = jnp.asarray(drawn.astype(out[name].dtype))
    for name, factor in factors.items():
        out[name] = (out[name] * factor).astype(out[name].dtype)
    return out
```

```python
from contextlib import ExitStack

import concourse.bass as bass
from concourse import mybir

ALU = mybir.AluOpType
ACT = mybir.ActivationFunctionType
F32 = mybir.dt.float32
BF16 = mybir.dt.bfloat16
I32 = mybir.dt.int32
AX_X = mybir.AxisListType.X

P = 128
N = 96
D = 1024
KT = D // P
HEADS = 16
HD = D // HEADS
EDGES = 1536
EC = EDGES // P
EXPERTS = 8
TYPES = 4
EPS = 1e-5
SCALE = 1.0 / HD ** 0.5
ABSENT = -1.0e30

WQ, WK, WIQ, WIK, WV, WIV, WO, W1, W2 = range(9)
MATS = 9
PER = 2
CPM = KT // PER
CHUNKS = MATS * CPM
RING = 16
ACC = 3


def gnn_ffn_kernel(nc, xT, weights, cols, edge_cols, edge_rows, type_weights, br, b2, out):
    ctx = ExitStack()
    with ctx:
        def sb(name, shape, dt=F32):
            return ctx.enter_context(nc.sbuf_tensor(name, shape, dt))

        def bank(name):
            return ctx.enter_context(nc.psum_tensor(name, [P, 512], F32))

        def sem(name):
            return ctx.enter_context(nc.semaphore(name))

        ring = sb("ring", [P, RING, PER, KT, P])
        x_sb = sb("x_sb", [P, KT, N])
        xc = sb("xc", [P, KT, N])
        sq = sb("sq", [P, KT, N])
        q = sb("q", [P, KT, N])
        k = sb("k", [P, KT, N])
        q2 = sb("q2", [P, KT, N])
        k2 = sb("k2", [P, KT, N])
        v, v2 = q, k
        v2n = sb("v2n", [N, KT, P])
        prob = sb("prob", [N, 4, 4, N])
        probT = sb("probT", [N, 4, 4, N])
        ao = sb("ao", [P, KT, N])
        x1 = sb("x1", [P, KT, N])
        early = sb("early", [P, 2, KT, N])
        hid = early[:, 0]
        res = early[:, 1]
        gate_diag = sb("gate_diag", [N, EXPERTS, N])
        part = sb("part", [P, 4, N])
        rstd = sb("rstd", [P, N])
        rscr = sb("rscr", [P, N])
        rstd_n = sb("rstd_n", [N, 1])
        rscr_n = sb("rscr_n", [N, 1])
        cols_sb = sb("cols_sb", [P, 8 + EXPERTS, 8])
        bias = cols_sb[:, 0:8, :]
        wr = cols_sb[:, 8:16, :]
        b2_sb = sb("b2_sb", [EXPERTS, D])
        br_sb = sb("br_sb", [N, EXPERTS])
        ident = sb("ident", [P, P])
        mean_w = sb("mean_w", [P, P])
        ones = sb("ones", [P, P])
        mhalf = sb("mhalf", [P, N])
        ecol = sb("ecol", [P, 3, EC], I32)
        ecol_f = sb("ecol_f", [P, 3, EC])
        erow = prob[0:2, :, :, :].rearrange("p g h n -> p (g h n)").bitcast(I32)
        erow_b = v2n[0:2, :, :].rearrange("p t d -> p (t d)").bitcast(BF16)[:, 0:EDGES]
        key_w = sb("key_w", [2, P], BF16)
        key_w_i = sb("key_w_i", [2, P], I32)
        keys = early[:, :, :, :].rearrange("p a t n -> p (a t n)")
        key_col = sb("key_col", [P, EC])
        later = sb("later", [P, P])
        same = x1[:, :, :].rearrange("p t n -> p (t n)").bitcast(BF16)
        dup = sb("dup", [P, 2, EC])
        code = sb("code", [P, EC])
        iota_i = sb("iota_i", [P, N], I32)
        iota_f = sb("iota_f", [P, N])
        src_hot = sb("src_hot", [P, EC, N], BF16)
        dst_hot = sb("dst_hot", [P, EC, N], BF16)
        cell = sb("cell", [N, N])
        cell_t = sb("cell_t", [N, N])
        mask = sb("mask", [N, N])
        tw = sb("tw", [N, 4, TYPES])
        smax = sb("smax", [N, 4, 4])
        ssum = sb("ssum", [N, 4, 4])
        sinv = sb("sinv", [N, 4, 4])
        logit = sb("logit", [N, EXPERTS])
        top = sb("top", [N, 8])
        ntop = sb("ntop", [N, 1])
        gate = sb("gate", [N, EXPERTS])
        gsum = sb("gsum", [N, 2])
        gateT = sb("gateT", [EXPERTS, N])

        acc = [bank(f"acc{i}") for i in range(ACC)]
        aux = [bank(f"aux{i}") for i in range(4)]
        stat = bank("stat")

        w_landed = [sem(f"w_landed{i}") for i in range(RING)]
        x_landed = sem("x_landed")
        cols_landed = sem("cols_landed")
        edges_landed = sem("edges_landed")
        rows_landed = sem("rows_landed")
        small_landed = sem("small_landed")
        const_done = sem("const_done")
        chunk_done = sem("chunk_done")
        evac = sem("evac")
        part_ready = sem("part_ready")
        mean_done = sem("mean_done")
        centered = sem("centered")
        squared = sem("squared")
        sq_ready = sem("sq_ready")
        var_done = sem("var_done")
        var_out = sem("var_out")
        rstd_ready = sem("rstd_ready")
        step = sem("step")
        pool_step = sem("pool_step")
        act_step = sem("act_step")
        rows_ready = sem("rows_ready")
        keys_done = sem("keys_done")
        keys_out = sem("keys_out")
        codes_ready = sem("codes_ready")
        src_ready = sem("src_ready")
        dst_ready = sem("dst_ready")
        cells_done = sem("cells_done")
        cells_out = sem("cells_out")
        tw_ready = sem("tw_ready")
        scores_done = sem("scores_done")
        scores_out = sem("scores_out")
        exped = sem("exped")
        prob_ready = sem("prob_ready")
        prob_normed = sem("prob_normed")
        probT_done = sem("probT_done")
        probT_out = sem("probT_out")
        v2n_done = sem("v2n_done")
        v2n_out = sem("v2n_out")
        heads_done = sem("heads_done")
        ao_out = sem("ao_out")
        logits_done = sem("logits_done")
        logits_ready = sem("logits_ready")
        gate_exped = sem("gate_exped")
        gate_ready = sem("gate_ready")
        gateT_done = sem("gateT_done")
        gateT_out = sem("gateT_out")
        diag_ready = sem("diag_ready")
        gate_rows_done = sem("gate_rows_done")
        scaled = sem("scaled")
        gelu_done = sem("gelu_done")
        hid_ready = sem("hid_ready")
        stored = sem("stored")

        block = ctx.enter_context(nc.Block())

        def half(t, p):
            return t[:, PER * p:PER * (p + 1), :]

        @block.sync
        def _(sp):
            sp.dma_start(x_sb[:, :, :], xT).then_inc(x_landed, 16)
            for c in range(CHUNKS):
                if c >= RING:
                    sp.wait_ge(chunk_done, c - RING + 1)
                sp.dma_start(ring[:, c % RING], weights[c]).then_inc(w_landed[c % RING], 16)
            for p in range(CPM):
                sp.wait_ge(evac, CPM * W2 + p + 1)
                sp.dma_start(out[:, PER * p:PER * (p + 1), :], half(res, p)).then_inc(stored, 16)
            sp.wait_ge(stored, 16 * CPM)

        @block.gpsimd
        def _(pool):
            pool.memset(mean_w[:, :], 1.0 / D).then_inc(const_done, 1)
            pool.memset(ones[:, :], 1.0).then_inc(const_done, 1)
            pool.memset(mhalf[:, :], -0.5).then_inc(const_done, 1)
            pool.memset(ident[:, :], 0.0).then_inc(pool_step, 1)
            pool.memset(later[:, :], 1.0).then_inc(pool_step, 1)
            pool.wait_ge(pool_step, 2)
            pool.affine_select(out=ident[:, :], in_=ident[:, :], compare_op=ALU.not_equal, fill=1.0, base=0,
                               pattern=[[-1, P]], channel_multiplier=1).then_inc(const_done, 1)
            pool.affine_select(out=later[:, :], in_=later[:, :], compare_op=ALU.is_gt, fill=0.0, base=0,
                               pattern=[[1, P]], channel_multiplier=-1).then_inc(const_done, 1)
            pool.iota(iota_i[:, :], pattern=[[1, N]], base=0, channel_multiplier=0).then_inc(pool_step, 1)
            pool.iota(key_w_i[:, :], pattern=[[0, P]], base=N, channel_multiplier=1 - N).then_inc(pool_step, 1)
            pool.wait_ge(pool_step, 4)
            pool.tensor_copy(key_w[:, :], key_w_i[:, :]).then_inc(const_done, 1)
            pool.tensor_copy(iota_f[:, :], iota_i[:, :]).then_inc(const_done, 1)
            pool.wait_ge(const_done, 7)
            pool.wait_ge(var_out, 2)
            pool.tensor_tensor(rstd[:, :], rscr[:, :], mhalf[:, :], ALU.pow).then_inc(rstd_ready, 1)
            pool.wait_ge(codes_ready, 1)
            for c in range(EC):
                last = pool.tensor_scalar(dst_hot[:, c], iota_f[:, :], ecol_f[:, 1, c:c + 1], code[:, c:c + 1],
                                          ALU.is_equal, ALU.mult)
            last.then_inc(dst_ready, 1)
            pool.wait_ge(var_out, 4)
            pool.tensor_tensor(rstd_n[:, :], rscr_n[:, :], mhalf[0:N, 0:1], ALU.pow).then_inc(rstd_ready, 1)
            pool.tensor_tensor(rstd[:, :], rscr[:, :], mhalf[:, :], ALU.pow).then_inc(rstd_ready, 1)

        @block.scalar
        def _(act):
            act.dma_start(cols_sb[:, :, :], cols).then_inc(cols_landed, 16)
            act.dma_start(ecol[:, :, :], edge_cols).then_inc(edges_landed, 16)
            act.dma_start(erow[:, :], edge_rows).then_inc(rows_landed, 16)
            act.dma_start(tw[:, 0, :], type_weights.to_broadcast([N, TYPES])).then_inc(small_landed, 16)
            act.dma_start(br_sb[:, :], br.to_broadcast([N, EXPERTS])).then_inc(small_landed, 16)
            act.dma_start(b2_sb[:, :], b2).then_inc(small_landed, 16)
            act.wait_ge(centered, 2)
            act.activation(sq[:, :, :], xc[:, :, :], ACT.Square).then_inc(squared, 1)
            act.wait_ge(small_landed, 48)
            act.activation(tw[:, 1, :], tw[:, 0, :], ACT.Abs).then_inc(act_step, 1)
            act.wait_ge(act_step, 1)
            act.activation(tw[:, 2, :], tw[:, 1, :], ACT.Exp, scale=-1.0).then_inc(act_step, 1)
            act.wait_ge(act_step, 2)
            act.activation(tw[:, 3, :], tw[:, 2, :], ACT.Ln, bias=1.0).then_inc(tw_ready, 1)
            for i in range(3):
                act.wait_ge(keys_done, i + 1)
                act.copy(keys[:, 512 * i:512 * (i + 1)], aux[i][:, :]).then_inc(keys_out, 1)
            for g in range(4):
                act.wait_ge(prob_ready, g + 1)
                act.activation(prob[:, g], prob[:, g], ACT.Exp).then_inc(exped, 1)
            for g in range(4):
                act.wait_ge(probT_done, g + 1)
                act.copy(probT[:, g], aux[g][0:N, 0:4 * N].rearrange("p (h n) -> p h n", h=4)).then_inc(probT_out, 1)
            act.wait_ge(centered, 4)
            act.activation(sq[:, :, :], xc[:, :, :], ACT.Square).then_inc(squared, 1)
            act.wait_ge(logits_ready, 1)
            act.activation(gate[:, :], logit[:, :], ACT.Exp, bias=ntop[:, :]).then_inc(gate_exped, 1)
            for e in range(EXPERTS):
                act.wait_ge(scaled, e // PER + 1)
                act.activation(hid[:, e], hid[:, e], ACT.Gelu, bias=bias[:, 7, e:e + 1]).then_inc(gelu_done, 1)

        @block.vector
        def _(dve):
            steps = [0]

            def then(ins):
                steps[0] += 1
                ins.then_inc(step, 1)
                dve.wait_ge(step, steps[0])

            def rows(ap, shape):
                return ap.to_broadcast(shape)

            def pair(c):
                return acc[c % ACC][:, 0:PER * N].rearrange("p (t n) -> p t n", t=PER)

            def biases(m, p):
                return bias[:, m, PER * p:PER * (p + 1)].unsqueeze(2).to_broadcast([P, PER, N])

            rstd_pair = rstd[:, :].unsqueeze(1).to_broadcast([P, PER, N])

            dve.wait_ge(x_landed, 16)
            dve.tensor_reduce(part[:, 0], x_sb[:, :, :].rearrange("p t n -> p n t"), axis=AX_X, op=ALU.add)\
                .then_inc(part_ready, 1)

            def center(x, base):
                dve.wait_ge(mean_done, base + 1)
                for i in range(2):
                    dve.tensor_tensor(xc[:, 4 * i:4 * i + 4], x[:, 4 * i:4 * i + 4],
                                      stat[:, 0:N].unsqueeze(1).to_broadcast([P, 4, N]), ALU.subtract)\
                        .then_inc(centered, 1)

            def sum_squares(n):
                dve.wait_ge(squared, n)
                dve.tensor_reduce(part[:, 1], sq[:, :, :].rearrange("p t n -> p n t"), axis=AX_X, op=ALU.add)\
                    .then_inc(sq_ready, 1)

            center(x_sb, 0)
            sum_squares(1)
            dve.wait_ge(var_done, 1)
            dve.tensor_scalar(rscr[:, :], stat[:, 128:128 + N], EPS, None, ALU.add).then_inc(var_out, 2)
            dve.wait_ge(cols_landed, 16)
            dve.wait_ge(centered, 2)
            then(dve.tensor_tensor(x_sb[:, :, :], x_sb[:, :, :],
                                   bias[:, 6, :].unsqueeze(2).to_broadcast([P, KT, N]), ALU.add))

            dve.wait_ge(rows_landed, 16)
            dve.tensor_copy(erow_b[:, :], erow[:, :]).then_inc(rows_ready, 1)
            dve.wait_ge(edges_landed, 16)
            then(dve.tensor_copy(ecol_f[:, :, :], ecol[:, :, :]))
            then(dve.tensor_scalar(code[:, :], ecol_f[:, 2, :], 0.0, float(TYPES), ALU.is_equal, ALU.mult))
            dve.tensor_tensor(code[:, :], code[:, :], ecol_f[:, 2, :], ALU.add).then_inc(codes_ready, 1)
            then(dve.scalar_tensor_tensor(key_col[:, :], ecol_f[:, 0, :], float(N), ecol_f[:, 1, :],
                                          ALU.mult, ALU.add))
            then(dve.memset(dup[:, :, :], 0.0))

            def evacuate(c):
                m, p = c // CPM, c % CPM
                dve.wait_ge(chunk_done, c + 1)
                if m in (WQ, WK, WV):
                    if c == 0:
                        dve.wait_ge(rstd_ready, 1)
                    to = {WQ: q, WK: k, WV: v}[m]
                    b = {WQ: 0, WK: 1, WV: 4}[m]
                    then(dve.tensor_tensor(half(to, p), pair(c), rstd_pair, ALU.mult))
                    dve.tensor_tensor(half(to, p), half(to, p), biases(b, p), ALU.add).then_inc(evac, 1)
                elif m in (WIQ, WIK, WIV):
                    to = {WIQ: q2, WIK: k2, WIV: v2}[m]
                    b = {WIQ: 2, WIK: 3, WIV: 5}[m]
                    dve.tensor_tensor(half(to, p), pair(c), biases(b, p), ALU.add).then_inc(evac, 1)
                elif m == WO:
                    dve.tensor_tensor(half(x1, p), pair(c), half(x_sb, p), ALU.add).then_inc(evac, 1)
                    dve.wait_ge(evac, c + 1)
                    ins = dve.tensor_tensor(part[:, 2] if p else part[:, 0], x1[:, 2 * p], x1[:, 2 * p + 1], ALU.add)
                    if p:
                        then(ins)
                        ins = dve.tensor_tensor(part[:, 0], part[:, 0], part[:, 2], ALU.add)
                    if p == CPM - 1:
                        ins.then_inc(part_ready, 1)
                    else:
                        then(ins)
                elif m == W1:
                    if p == 0:
                        dve.wait_ge(rstd_ready, 3)
                    dve.tensor_tensor(half(hid, p), pair(c), rstd_pair, ALU.mult).then_inc(evac, 1)
                    dve.wait_ge(evac, c + 1)
                    dve.engine_nop().then_inc(scaled, 1)
                else:
                    dve.tensor_tensor(half(res, p), pair(c), half(x1, p), ALU.add).then_inc(evac, 1)

            def count_later(c):
                if c < EC - 1:
                    dve.tensor_scalar(same[:, P * (c + 1):], keys[:, P * (c + 1):], key_col[:, c:c + 1], 0.0,
                                      ALU.is_equal, ALU.add, accum_out=dup[:, 0, c:c + 1])
                then(dve.scalar_tensor_tensor(same[:, P * c:P * (c + 1)], keys[:, P * c:P * (c + 1)],
                                              key_col[:, c:c + 1], later[:, :], ALU.is_equal, ALU.mult,
                                              accum_out=dup[:, 1, c:c + 1]))

            def one_hot_sources():
                then(dve.tensor_tensor(dup[:, 0], dup[:, 0], dup[:, 1], ALU.add))
                then(dve.scalar_tensor_tensor(dup[:, 1], dup[:, 0], float(P), ecol_f[:, 0, :], ALU.mult, ALU.add))
                dve.tensor_tensor(src_hot[:, :, :], iota_f[:, :].unsqueeze(1).to_broadcast([P, EC, N]),
                                  dup[:, 1, :].unsqueeze(2).to_broadcast([P, EC, N]), ALU.is_equal)\
                    .then_inc(src_ready, 1)

            def build_mask():
                dve.wait_ge(tw_ready, 1)
                then(dve.scalar_tensor_tensor(tw[:, 1, :], tw[:, 0, :], 0.0, tw[:, 3, :], ALU.max, ALU.add))
                dve.wait_ge(cells_done, 1)
                then(dve.scalar_tensor_tensor(cell_t[:, :], aux[3][0:N, 0:N], 0.0, ident[0:N, 0:N],
                                              ALU.is_equal, ALU.mult))
                then(dve.scalar_tensor_tensor(cell[:, :], cell_t[:, :], float(TYPES), aux[3][0:N, 0:N],
                                              ALU.mult, ALU.add))
                then(dve.tensor_scalar(mask[:, :], cell[:, :], 0.0, ABSENT, ALU.is_equal, ALU.mult))
                for t in range(TYPES):
                    then(dve.tensor_scalar(cell_t[:, :], cell[:, :], float(t + 1), tw[:, 1, t:t + 1],
                                           ALU.is_equal, ALU.mult))
                    then(dve.tensor_tensor(mask[:, :], mask[:, :], cell_t[:, :], ALU.add))

            def scores(g):
                dve.wait_ge(scores_done, g // 2 + 1)
                s = prob[:, g]
                dve.scalar_tensor_tensor(s, aux[g][0:N, 0:4 * N].rearrange("p (h n) -> p h n", h=4), SCALE,
                                         mask[:, :].unsqueeze(1).to_broadcast([N, 4, N]), ALU.mult, ALU.add)\
                    .then_inc(scores_out, 1)
                dve.wait_ge(scores_out, g + 1)
                then(dve.tensor_reduce(smax[:, g], s, axis=AX_X, op=ALU.max))
                dve.tensor_tensor(s, s, smax[:, g].unsqueeze(2).to_broadcast([N, 4, N]), ALU.subtract)\
                    .then_inc(prob_ready, 1)

            def normalise(g):
                dve.wait_ge(exped, g + 1)
                s = prob[:, g]
                then(dve.tensor_reduce(ssum[:, g], s, axis=AX_X, op=ALU.add))
                then(dve.reciprocal(sinv[:, g], ssum[:, g]))
                dve.tensor_tensor(s, s, sinv[:, g].unsqueeze(2).to_broadcast([N, 4, N]), ALU.mult)\
                    .then_inc(prob_normed, 1)

            for c in range(CPM * WV):
                evacuate(c)
                if 1 <= c <= 6:
                    if c == 1:
                        dve.wait_ge(keys_out, 3)
                        dve.wait_ge(const_done, 7)
                    count_later(2 * c - 2)
                    count_later(2 * c - 1)
                if c == 7:
                    one_hot_sources()
                if c == 10:
                    build_mask()
            evacuate(16)
            scores(0)
            scores(1)
            evacuate(17)
            normalise(0)
            scores(2)
            evacuate(18)
            normalise(1)
            scores(3)
            evacuate(19)
            normalise(2)
            normalise(3)
            for c in range(20, 24):
                evacuate(c)
            for i in range(2):
                dve.wait_ge(v2n_done, i + 1)
                dve.tensor_copy(v2n[:, 4 * i:4 * i + 4], acc[i][0:N, :].rearrange("p (t d) -> p t d", t=4))\
                    .then_inc(v2n_out, 1)
            for i in range(2):
                dve.wait_ge(heads_done, i + 1)
                dve.tensor_copy(ao[:, 4 * i:4 * i + 4], aux[i][:, 0:4 * N].rearrange("p (t n) -> p t n", t=4))\
                    .then_inc(ao_out, 1)
            for c in range(24, 28):
                evacuate(c)
            center(x1, 1)
            sum_squares(2)
            dve.wait_ge(var_done, 2)
            dve.tensor_scalar(rscr_n[:, :], stat[0:N, 256:257], EPS, None, ALU.add).then_inc(var_out, 1)
            dve.tensor_scalar(rscr[:, :], stat[:, 128:128 + N], EPS, None, ALU.add).then_inc(var_out, 1)
            dve.wait_ge(logits_done, 1)
            dve.wait_ge(small_landed, 48)
            dve.wait_ge(rstd_ready, 2)
            then(dve.scalar_tensor_tensor(logit[:, :], aux[2][0:N, 0:EXPERTS], rstd_n[:, :], br_sb[:, :],
                                          ALU.mult, ALU.add))
            then(dve.max(top[:, :], logit[:, :]))
            dve.tensor_scalar(ntop[:, :], top[:, 0:1], -1.0, None, ALU.mult).then_inc(logits_ready, 1)
            dve.wait_ge(gate_exped, 1)
            then(dve.scalar_tensor_tensor(gate[:, :], logit[:, :], top[:, 1:2], gate[:, :], ALU.is_ge, ALU.mult))
            then(dve.tensor_reduce(gsum[:, 0:1], gate[:, :], axis=AX_X, op=ALU.add))
            then(dve.reciprocal(gsum[:, 1:2], gsum[:, 0:1]))
            dve.tensor_scalar(gate[:, :], gate[:, :], gsum[:, 1:2], None, ALU.mult).then_inc(gate_ready, 1)
            dve.wait_ge(gate_ready, 1)
            dve.tensor_tensor(gate_diag[:, :, :], ident[0:N, 0:N].unsqueeze(1).to_broadcast([N, EXPERTS, N]),
                              gate[:, :].unsqueeze(2).to_broadcast([N, EXPERTS, N]), ALU.mult)\
                .then_inc(diag_ready, 1)
            dve.wait_ge(gateT_done, 1)
            dve.tensor_copy(gateT[:, :], aux[3][0:EXPERTS, 0:N]).then_inc(gateT_out, 1)

            def weigh(p):
                dve.wait_ge(gelu_done, PER * (p + 1))
                if p == 0:
                    dve.wait_ge(gate_rows_done, 1)
                rows_ = aux[p // 2][:, 0:4 * N].rearrange("p (t n) -> p t n", t=4)
                dve.tensor_tensor(half(hid, p), half(hid, p), rows_[:, PER * (p % 2):PER * (p % 2) + PER], ALU.mult)\
                    .then_inc(hid_ready, 1)

            evacuate(28)
            evacuate(29)
            weigh(0)
            evacuate(30)
            weigh(1)
            evacuate(31)
            weigh(2)
            weigh(3)
            for c in range(32, 36):
                evacuate(c)

        @block.tensor
        def _(pe):
            def chunk(c, rhs, ready, pieces=1):
                pe.wait_ge(w_landed[c % RING], 16 * (c // RING + 1))
                if c >= ACC:
                    pe.wait_ge(evac, c - ACC + 1)
                last = None
                for t in range(PER):
                    first = True
                    if c // CPM == W2:
                        tile = PER * (c % CPM) + t
                        nc.tensor.matmul(acc[c % ACC][:, N * t:N * (t + 1)], b2_sb[:, P * tile:P * (tile + 1)],
                                         gateT[:, :], start=True, stop=False)
                        first = False
                    for kt in range(KT):
                        if t == 0:
                            ready(kt)
                        last = nc.tensor.matmul(acc[c % ACC][:, N * t:N * (t + 1)], ring[:, c % RING, t, kt],
                                                rhs[:, kt], start=(first and kt == 0), stop=(kt == KT - 1))
                last.then_inc(chunk_done, 1)

            def matrix(m, rhs, made_by):
                def ready(kt):
                    if c == CPM * m and kt % PER == 0:
                        pe.wait_ge(evac, CPM * made_by + kt // PER + 1)
                for c in range(CPM * m, CPM * (m + 1)):
                    chunk(c, rhs, ready)

            def nothing(kt):
                pass

            def statistics(n):
                pe.wait_ge(sq_ready, n)
                last = nc.tensor.matmul(stat[:, 128:128 + N], mean_w[:, :], part[:, 1], start=True, stop=True)
                if n == 2:
                    last = nc.tensor.matmul(stat[0:N, 256:257], part[:, 1], mean_w[:, 0:1], start=True, stop=True)
                last.then_inc(var_done, 1)

            pe.wait_ge(const_done, 7)
            pe.wait_ge(part_ready, 1)
            nc.tensor.matmul(stat[:, 0:N], mean_w[:, :], part[:, 0], start=True, stop=True).then_inc(mean_done, 1)

            def ready_centered(kt):
                if kt % 4 == 0:
                    pe.wait_ge(centered, kt // 4 + 1)

            chunk(0, xc, ready_centered)
            statistics(1)
            pe.wait_ge(rows_ready, 1)
            for i in range(3):
                nc.tensor.matmul(aux[i][:, :], key_w[:, :], erow_b[:, 512 * i:512 * (i + 1)],
                                 start=True, stop=True).then_inc(keys_done, 1)
            for c in range(1, CPM * 2):
                chunk(c, xc, nothing)
            matrix(WIQ, q, WQ)
            pe.wait_ge(src_ready, 1)
            pe.wait_ge(dst_ready, 1)
            for c in range(EC):
                last = nc.tensor.matmul(aux[3][0:N, 0:N], src_hot[:, c], dst_hot[:, c],
                                        start=(c == 0), stop=(c == EC - 1))
            last.then_inc(cells_done, 1)
            matrix(WIK, k, WK)
            chunk(16, xc, nothing)
            pe.wait_ge(evac, CPM * (WIK + 1))
            for h in range(HEADS):
                g, i, s = 2 * (h // 8) + h % 2, (h % 8) // 2, HD * (h % 2)
                last = nc.tensor.matmul(aux[g][0:N, N * i:N * (i + 1)], q2[s:s + HD, h // 2], k2[s:s + HD, h // 2],
                                        start=True, stop=True)
                if h % 8 == 7:
                    last.then_inc(scores_done, 1)
            for c in range(17, 20):
                chunk(c, xc, nothing)
            matrix(WIV, v, WV)

            def transpose_probs(g):
                pe.wait_ge(prob_normed, g + 1)
                for i in range(4):
                    last = nc.tensor.transpose(aux[g][0:N, N * i:N * (i + 1)], prob[:, g, i], ident[0:N, 0:N])
                last.then_inc(probT_done, 1)

            for g in range(4):
                transpose_probs(g)
            for i in range(2):
                pe.wait_ge(evac, CPM * WIV + 2 * i + 2)
                if i == 0:
                    pe.wait_ge(evac, CPM * WIV + 4)
                for t in range(4):
                    last = nc.tensor.transpose(acc[i][0:N, P * t:P * (t + 1)], v2[:, 4 * i + t], ident[:, :])
                last.then_inc(v2n_done, 1)
            for i in range(2):
                pe.wait_ge(v2n_out, i + 1)
                if i == 0:
                    pe.wait_ge(probT_out, 4)
                for t in range(4):
                    for s in range(2):
                        h = 2 * (4 * i + t) + s
                        g, j = 2 * (h // 8) + h % 2, (h % 8) // 2
                        last = nc.tensor.matmul(aux[i][HD * s:HD * (s + 1), N * t:N * (t + 1)],
                                                v2n[:, 4 * i + t, HD * s:HD * (s + 1)], probT[:, g, j],
                                                start=True, stop=True)
                last.then_inc(heads_done, 1)

            def ready_ao(kt):
                if c == CPM * WO and kt % 4 == 0:
                    pe.wait_ge(ao_out, kt // 4 + 1)

            for c in range(24, 28):
                chunk(c, ao, ready_ao)
            pe.wait_ge(part_ready, 2)
            nc.tensor.matmul(stat[:, 0:N], mean_w[:, :], part[:, 0], start=True, stop=True).then_inc(mean_done, 1)

            def ready_centered2(kt):
                if kt % 4 == 0:
                    pe.wait_ge(centered, kt // 4 + 3)

            chunk(28, xc, ready_centered2)
            for kt in range(KT):
                last = nc.tensor.matmul(aux[2][0:N, 0:EXPERTS], xc[:, kt], wr[:, kt], start=(kt == 0), stop=(kt == KT - 1))
            last.then_inc(logits_done, 1)
            statistics(2)
            chunk(29, xc, nothing)
            chunk(30, xc, nothing)
            pe.wait_ge(gate_ready, 1)
            nc.tensor.transpose(aux[3][0:EXPERTS, 0:N], gate[:, :], ident[0:N, 0:N]).then_inc(gateT_done, 1)
            pe.wait_ge(diag_ready, 1)
            for i in range(2):
                last = nc.tensor.matmul(aux[i][:, 0:4 * N], ones[0:N, :],
                                        gate_diag[:, 4 * i:4 * i + 4].rearrange("p e n -> p (e n)"), start=True, stop=True)
            last.then_inc(gate_rows_done, 1)
            chunk(31, xc, nothing)

            pe.wait_ge(gateT_out, 1)
            pe.wait_ge(small_landed, 48)

            def ready_hid(kt):
                if c == CPM * W2 and kt % PER == 0:
                    pe.wait_ge(hid_ready, kt // PER + 1)

            for c in range(32, 36):
                chunk(c, hid, ready_hid)


def kernel(x, src, dst, edge_type_5, L0_gnn_edge_type_weights, L0_gnn_wq, L0_gnn_bq, L0_gnn_wk, L0_gnn_bk, L0_gnn_wv,
           L0_gnn_bv, L0_gnn_wiq, L0_gnn_biq, L0_gnn_wik, L0_gnn_bik, L0_gnn_wiv, L0_gnn_biv, L0_gnn_wo, L0_gnn_bo,
           L0_ffn_W1, L0_ffn_b1, L0_ffn_W2, L0_ffn_b2, L0_ffn_Wr, L0_ffn_br):
    import numpy as np
    import concourse.bacc as bacc
    from concourse.bass_utils import run_bass_kernel_spmd

    a = np.asarray

    def tiles(w_out_in):
        w = a(w_out_in).reshape(CPM, PER, P, KT, P)
        return w.transpose(0, 4, 1, 3, 2)

    w1 = a(L0_ffn_W1).reshape(CPM, PER, KT, P, P).transpose(0, 3, 1, 2, 4)
    w2 = a(L0_ffn_W2).reshape(EXPERTS, P, CPM, PER, P).transpose(2, 1, 3, 0, 4)
    mats = [tiles(w) for w in (L0_gnn_wq, L0_gnn_wk, L0_gnn_wiq, L0_gnn_wik, L0_gnn_wv, L0_gnn_wiv, L0_gnn_wo)]
    weights = np.ascontiguousarray(np.concatenate(mats + [w1, w2]))
    xT = np.ascontiguousarray(a(x).T.reshape(KT, P, N).transpose(1, 0, 2))
    biases = np.stack([a(b).reshape(8, P) for b in (L0_gnn_bq, L0_gnn_bk, L0_gnn_biq, L0_gnn_bik, L0_gnn_bv, L0_gnn_biv,
                                                    L0_gnn_bo, L0_ffn_b1)])
    router = a(L0_ffn_Wr).reshape(KT, P, EXPERTS)
    cols = np.ascontiguousarray(np.concatenate([biases.transpose(2, 0, 1), router.transpose(1, 0, 2)], axis=1))
    edges = np.stack([a(e) for e in (src, dst, edge_type_5)])
    arrays = {
        "xT": xT,
        "weights": weights,
        "cols": cols,
        "edge_cols": np.ascontiguousarray(edges.reshape(3, EC, P).transpose(2, 0, 1)),
        "edge_rows": np.ascontiguousarray(edges[0:2]),
        "type_weights": a(L0_gnn_edge_type_weights).reshape(1, TYPES),
        "br": a(L0_ffn_br).reshape(1, EXPERTS),
        "b2": np.ascontiguousarray(a(L0_ffn_b2)),
    }
    nc = bacc.Bacc("TRN2", target_bir_lowering=False, num_devices=1)
    args = [nc.dram_tensor(n, v.shape, mybir.dt.from_np(v.dtype), kind="ExternalInput").ap() for n, v in arrays.items()]
    args.append(nc.dram_tensor("outT", (P, KT, N), F32, kind="ExternalOutput").ap())
    gnn_ffn_kernel(nc, *args)
    r = run_bass_kernel_spmd(nc, [arrays], core_ids=[0])
    got = r.results[0]["outT"]
    return np.ascontiguousarray(got.transpose(2, 1, 0).reshape(N, D))
```

```python
from contextlib import ExitStack

import concourse.bass as bass
from concourse import mybir

ALU = mybir.AluOpType
ACT = mybir.ActivationFunctionType
F32 = mybir.dt.float32
F32R = mybir.dt.float32r
BF16 = mybir.dt.bfloat16
I32 = mybir.dt.int32
AX_X = mybir.AxisListType.X

P = 128
N = 96
D = 1024
KT = D // P
HEADS = 16
HD = D // HEADS
EDGES = 1536
EC = EDGES // P
EXPERTS = 8
TYPES = 4
EPS = 1e-5
SCALE = 1.0 / HD ** 0.5
ABSENT = -1.0e30

WQ, WK, WIQ, WIK, WV, WIV, WO, W1, W2 = range(9)
MATS = 9
STATIONARY = 5
PER = 2
HALF = D // 2
KG = KT // 2
CPM = 4
CHUNKS = MATS * CPM
NAT = STATIONARY * CPM
FIRST_SPLIT = NAT + 2
RING = 6
PARTS = 6
WARM = 11
WARM_2 = 4
ACC = 3


def gnn_ffn_kernel(nc, xT, x, weights, cols, edge_cols, edge_rows, type_weights, bo, b1, br, b2, out):
    ctx = ExitStack()
    with ctx:
        def sb(name, shape, dt=F32):
            return ctx.enter_context(nc.sbuf_tensor(name, shape, dt))

        def bank(name):
            return ctx.enter_context(nc.psum_tensor(name, [P, 512], F32))

        def sem(name):
            return ctx.enter_context(nc.semaphore(name))

        ring = sb("ring", [P, RING, KG, HALF])
        w_hi = sb("w_hi", [P, PARTS, KG, HALF], F32R)
        w_lo = sb("w_lo", [P, PARTS, KG, HALF], F32R)
        xc = sb("xc", [P, KT, N])
        q = sb("q", [P, KT, N])
        k = sb("k", [P, KT, N])
        q2 = sb("q2", [P, KT, N])
        k2 = sb("k2", [P, KT, N])
        x_sb, sq = q2, k2
        v = q
        ao = k
        xnT = q
        a_hi = sb("a_hi", [P, KT, N], F32R)
        a_lo = sb("a_lo", [P, KT, N], F32R)
        g_hi = sb("g_hi", [P, KT, N], F32R)
        g_lo = sb("g_lo", [P, KT, N], F32R)
        v2n = sb("v2n", [N, HEADS, HD])
        prob = sb("prob", [P, 4, 4, N])
        probT = sb("probT", [P, 4, 4, N])
        x1_all = sb("x1_all", [P, D])
        x1 = x1_all[0:N, :]
        hid_all = sb("hid_all", [P, D])
        hid = hid_all[0:N, :]
        res = v2n[:, :, :].rearrange("p h d -> p (h d)")
        b1_all = sb("b1_all", [P, D])
        b1_sb = b1_all[0:N, :]
        stats = sb("stats", [N, 2, 6])
        moments = sb("moments", [N, 2])
        part = sb("part", [P, 2, N])
        rstd = sb("rstd", [P, N])
        rscr_n = sb("rscr_n", [N, 2])
        rstd_n = sb("rstd_n", [N, 2])
        rdiag = sb("rdiag", [N, N])
        cols_sb = sb("cols_sb", [P, 6 + EXPERTS, 8])
        bias = cols_sb[:, 0:6, :]
        wr = cols_sb[:, 6:14, :]
        b2_sb = prob[0:EXPERTS, :, :, :].rearrange("p g h n -> p (g h n)")[:, 0:D]
        br_sb = sb("br_sb", [N, EXPERTS])
        ident = sb("ident", [P, P])
        mean_w = sb("mean_w", [P, P])
        ones = sb("ones", [N, P])
        mhalf = sb("mhalf", [N, 1])
        ecol = sb("ecol", [P, 3, EC], I32)
        ecol_f = sb("ecol_f", [P, 3, EC])
        erow = probT[0:2, :, :, :].rearrange("p g h n -> p (g h n)").bitcast(I32)
        erow_b = v2n[0:2, :, :].rearrange("p h d -> p (h d)").bitcast(BF16)[:, 0:EDGES]
        key_w = sb("key_w", [2, P], BF16)
        key_w_i = sb("key_w_i", [2, P], I32)
        keys = prob[:, :, :, :].rearrange("p g h n -> p (g h n)")
        key_col = sb("key_col", [P, EC])
        later = x1_all[:, 0:P]
        same = k2[:, :, :].rearrange("p t n -> p (t n)").bitcast(BF16)
        dup = sb("dup", [P, 2, EC])
        code = sb("code", [P, EC])
        iota_i = x1_all[:, P:P + N].bitcast(I32)
        iota_f = x1_all[:, P + N:P + 2 * N]
        src_hot = k2[:, :, :].rearrange("p t n -> p (t n)").bitcast(BF16)[:, 0:EC * N].rearrange("p (c n) -> p c n", c=EC)
        dst_hot = hid_all[:, :].bitcast(BF16)[:, 0:EC * N].rearrange("p (c n) -> p c n", c=EC)
        cell = sb("cell", [N, N])
        cell_t = sb("cell_t", [N, N])
        mask = sb("mask", [N, N])
        tw = sb("tw", [N, 4, TYPES])
        smax = sb("smax", [N, 4, 4])
        ssum = sb("ssum", [N, 4, 4])
        sinv = sb("sinv", [N, 4, 4])
        logit = sb("logit", [N, EXPERTS])
        top = sb("top", [N, 8])
        ntop = sb("ntop", [N, 1])
        gate = sb("gate", [N, EXPERTS])
        gsum = sb("gsum", [N, 2])
        gateT = sb("gateT", [EXPERTS, N])

        warm = b1_all[:, 0:256].bitcast(BF16)

        acc = [bank(f"acc{i}") for i in range(ACC)]
        aux = [bank(f"aux{i}") for i in range(4)]
        stat = bank("stat")

        w_landed = [sem(f"w_landed{i}") for i in range(RING)]
        x_landed = sem("x_landed")
        xn_landed = sem("xn_landed")
        cols_landed = sem("cols_landed")
        edges_landed = sem("edges_landed")
        rows_landed = sem("rows_landed")
        small_landed = sem("small_landed")
        b2_landed = sem("b2_landed")
        const_done = sem("const_done")
        warm_ready = sem("warm_ready")
        chunk_done = sem("chunk_done")
        evac = sem("evac")
        hi_done = sem("hi_done")
        lo_done = sem("lo_done")
        part_ready = sem("part_ready")
        mean_done = sem("mean_done")
        centered = sem("centered")
        squared = sem("squared")
        sq_ready = sem("sq_ready")
        var_done = sem("var_done")
        var_out = sem("var_out")
        rstd_n_ready = sem("rstd_n_ready")
        rdiag_ready = sem("rdiag_ready")
        rstd_done = sem("rstd_done")
        xb_ready = sem("xb_ready")
        step = sem("step")
        pool_step = sem("pool_step")
        act_step = sem("act_step")
        rows_ready = sem("rows_ready")
        keys_done = sem("keys_done")
        keys_out = sem("keys_out")
        codes_ready = sem("codes_ready")
        src_ready = sem("src_ready")
        dst_ready = sem("dst_ready")
        cells_done = sem("cells_done")
        tw_ready = sem("tw_ready")
        scores_done = sem("scores_done")
        scores_out = sem("scores_out")
        prob_ready = sem("prob_ready")
        exped = sem("exped")
        prob_normed = sem("prob_normed")
        probT_done = sem("probT_done")
        probT_out = sem("probT_out")
        v_hi = sem("v_hi")
        v_lo = sem("v_lo")
        v2n_out = sem("v2n_out")
        heads_done = sem("heads_done")
        ao_ready = sem("ao_ready")
        ao_hi = sem("ao_hi")
        ao_lo = sem("ao_lo")
        x1_ready = sem("x1_ready")
        normed = sem("normed")
        xnT_done = sem("xnT_done")
        xn_hi = sem("xn_hi")
        xnT_out = sem("xnT_out")
        xn_lo = sem("xn_lo")
        logits_done = sem("logits_done")
        logits_ready = sem("logits_ready")
        gate_exped = sem("gate_exped")
        gate_ready = sem("gate_ready")
        gateT_done = sem("gateT_done")
        gateT_out = sem("gateT_out")
        hid_ready = sem("hid_ready")
        gelu_done = sem("gelu_done")
        weighed = sem("weighed")
        hidT_done = sem("hidT_done")
        hid_hi = sem("hid_hi")
        hid_lo = sem("hid_lo")
        res_ready = sem("res_ready")
        stored = sem("stored")

        block = ctx.enter_context(nc.Block())

        def half(t, p):
            return t[:, PER * p:PER * (p + 1), :]

        def quad(t, i):
            return t[:, KG * i:KG * (i + 1), :]

        def cut(t, i):
            return t[:, HALF * i:HALF * (i + 1)]

        def quad_psum(b):
            return b[:, 0:KG * N].rearrange("p (t n) -> p t n", t=KG)

        nat_bank = {(m, h): [acc[0], acc[1], acc[2], stat][2 * (m % 2 == 0) + h] for m in (WIV, WO, W1, W2) for h in (0, 1)}

        def chunk_of(c):
            return c // CPM, c % CPM // 2, c % 2

        @block.sync
        def _(sp):
            sp.dma_start(x_sb[:, :, :], xT).then_inc(x_landed, 16)
            for c in range(CHUNKS):
                if c >= RING:
                    old = c - RING
                    if old < FIRST_SPLIT:
                        sp.wait_ge(chunk_done, old + 1)
                    else:
                        sp.wait_ge(lo_done, old - FIRST_SPLIT + 1)
                sp.dma_start(ring[:, c % RING], weights[c]).then_inc(w_landed[c % RING], 16)
            for i in range(3):
                sp.wait_ge(res_ready, i + 1)
                lo, hi = (0, HALF, 3 * HALF // 2, D)[i:i + 2]
                sp.dma_start(out[:, lo:hi], res[:, lo:hi]).then_inc(stored, 16)
            sp.wait_ge(stored, 16 * 3)

        @block.gpsimd
        def _(pool):
            pool.memset(warm[:, :], 0.0).then_inc(warm_ready, 1)
            pool.memset(mean_w[:, :], 1.0 / D).then_inc(const_done, 1)
            pool.memset(ones[:, :], 1.0).then_inc(const_done, 1)
            pool.memset(mhalf[:, :], -0.5).then_inc(const_done, 1)
            pool.memset(ident[:, :], 0.0).then_inc(pool_step, 1)
            pool.memset(later[:, :], 1.0).then_inc(pool_step, 1)
            pool.wait_ge(pool_step, 2)
            pool.affine_select(out=ident[:, :], in_=ident[:, :], compare_op=ALU.not_equal, fill=1.0, base=0,
                               pattern=[[-1, P]], channel_multiplier=1).then_inc(const_done, 1)
            pool.affine_select(out=later[:, :], in_=later[:, :], compare_op=ALU.is_gt, fill=0.0, base=0,
                               pattern=[[1, P]], channel_multiplier=-1).then_inc(const_done, 1)
            pool.iota(iota_i[:, :], pattern=[[1, N]], base=0, channel_multiplier=0).then_inc(pool_step, 1)
            pool.iota(key_w_i[:, :], pattern=[[0, P]], base=N, channel_multiplier=1 - N).then_inc(pool_step, 1)
            pool.wait_ge(pool_step, 4)
            pool.tensor_copy(key_w[:, :], key_w_i[:, :]).then_inc(const_done, 1)
            pool.tensor_copy(iota_f[:, :], iota_i[:, :]).then_inc(const_done, 1)
            pool.wait_ge(const_done, 7)
            pool.wait_ge(var_out, 1)
            pool.tensor_tensor(rstd_n[:, 0:1], rscr_n[:, 0:1], mhalf[:, :], ALU.pow).then_inc(rstd_n_ready, 1)
            pool.wait_ge(codes_ready, 1)
            for c in range(EC):
                last = pool.tensor_scalar(dst_hot[:, c], iota_f[:, :], ecol_f[:, 1, c:c + 1], code[:, c:c + 1],
                                          ALU.is_equal, ALU.mult)
            last.then_inc(dst_ready, 1)
            pool.wait_ge(xn_landed, 32)
            pool.tensor_tensor(x1[:, :], x1[:, :], hid[:, :], ALU.add).then_inc(xb_ready, 1)
            pool.wait_ge(var_out, 2)
            pool.tensor_tensor(rstd_n[:, 1:2], rscr_n[:, 1:2], mhalf[:, :], ALU.pow).then_inc(rstd_n_ready, 1)

        @block.scalar
        def _(act):
            act.dma_start(cols_sb[:, :, :], cols).then_inc(cols_landed, 16)
            act.dma_start(ecol[:, :, :], edge_cols).then_inc(edges_landed, 16)
            act.dma_start(erow[:, :], edge_rows).then_inc(rows_landed, 16)
            act.dma_start(tw[:, 0, :], type_weights.to_broadcast([N, TYPES])).then_inc(small_landed, 16)
            act.dma_start(br_sb[:, :], br.to_broadcast([N, EXPERTS])).then_inc(small_landed, 16)
            act.wait_ge(centered, 2)
            act.activation(sq[:, :, :], xc[:, :, :], ACT.Square).then_inc(squared, 1)
            for i in range(3):
                act.wait_ge(keys_done, i + 1)
                act.copy(keys[:, 512 * i:512 * (i + 1)], aux[i][:, :]).then_inc(keys_out, 1)
            act.wait_ge(small_landed, 32)
            act.activation(tw[:, 1, :], tw[:, 0, :], ACT.Abs).then_inc(act_step, 1)
            act.wait_ge(act_step, 1)
            act.activation(tw[:, 2, :], tw[:, 1, :], ACT.Exp, scale=-1.0).then_inc(act_step, 1)
            act.wait_ge(act_step, 2)
            act.activation(tw[:, 3, :], tw[:, 2, :], ACT.Ln, bias=1.0).then_inc(tw_ready, 1)

            act.wait_ge(cells_done, 1)
            act.dma_start(x1[:, :], x).then_inc(xn_landed, 16)
            act.dma_start(hid[:, :], bo.to_broadcast([N, D])).then_inc(xn_landed, 16)
            act.dma_start(b1_sb[:, :], b1.to_broadcast([N, D])).then_inc(small_landed, 16)

            def split_hi(c):
                act.wait_ge(w_landed[c % RING], 16 * (c // RING + 1))
                if c - PARTS >= FIRST_SPLIT:
                    act.wait_ge(chunk_done, c - PARTS + 1)
                act.copy(w_hi[:, c % PARTS], ring[:, c % RING]).then_inc(hi_done, 1)

            def softmax_exp(g):
                act.wait_ge(prob_ready, g + 1)
                act.activation(prob[0:N, g], prob[0:N, g], ACT.Exp).then_inc(exped, 1)

            def gelu(i):
                act.wait_ge(hid_ready, i + 1)
                act.activation(cut(hid, i), cut(hid, i), ACT.Gelu).then_inc(gelu_done, 1)

            def hidden_hi(i):
                act.wait_ge(hidT_done, i + 1)
                act.copy(quad(g_hi, i), quad_psum(aux[i])).then_inc(hid_hi, 1)

            softmax_exp(0)
            softmax_exp(1)
            softmax_exp(2)
            softmax_exp(3)
            split_hi(22)
            act.wait_ge(evac, CPM * WV + 4)
            act.copy(quad(a_hi, 1), quad(v, 1)).then_inc(v_hi, 1)
            split_hi(23)
            split_hi(24)
            split_hi(25)
            act.wait_ge(chunk_done, 23)
            act.copy(v2n[:, 0:8], nat_bank[WIV, 0][0:N, :].rearrange("p (h d) -> p h d", h=8)).then_inc(v2n_out, 1)
            split_hi(26)
            for g in range(4):
                act.wait_ge(probT_done, g + 1)
                act.copy(probT[0:N, g], aux[g][0:N, 0:4 * N].rearrange("p (h n) -> p h n", h=4)).then_inc(probT_out, 1)
            act.wait_ge(chunk_done, 24)
            act.copy(v2n[:, 8:16], nat_bank[WIV, 1][0:N, :].rearrange("p (h d) -> p h d", h=8)).then_inc(v2n_out, 1)
            act.dma_start(b2_sb, b2).then_inc(b2_landed, 16)
            for i in range(2):
                act.wait_ge(ao_ready, i + 1)
                act.copy(quad(a_hi, i), quad(ao, i)).then_inc(ao_hi, 1)
            for c in range(27, 32):
                split_hi(c)
            for i in range(2):
                act.wait_ge(xnT_done, i + 1)
                act.copy(quad(a_hi, i), quad_psum(aux[i])).then_inc(xn_hi, 1)
            for i in range(2):
                act.wait_ge(xn_lo, i + 1)
                act.copy(quad(xnT, i), quad_psum(aux[i])).then_inc(xnT_out, 1)
            split_hi(32)
            split_hi(33)
            act.wait_ge(logits_ready, 1)
            act.activation(gate[:, :], logit[:, :], ACT.Exp, bias=ntop[:, :]).then_inc(gate_exped, 1)
            split_hi(34)
            gelu(0)
            hidden_hi(0)
            gelu(1)
            hidden_hi(1)
            split_hi(35)

        @block.vector
        def _(dve):
            steps = [0]

            def then(ins):
                steps[0] += 1
                ins.then_inc(step, 1)
                dve.wait_ge(step, steps[0])

            def pair(c):
                return acc[c % ACC][:, 0:PER * N].rearrange("p (t n) -> p t n", t=PER)

            def biases(m, p):
                return bias[:, m, PER * p:PER * (p + 1)].unsqueeze(2).to_broadcast([P, PER, N])

            rstd_pair = rstd[:, :].unsqueeze(1).to_broadcast([P, PER, N])

            dve.wait_ge(x_landed, 16)
            dve.tensor_reduce(part[:, 0], x_sb[:, :, :].rearrange("p t n -> p n t"), axis=AX_X, op=ALU.add)\
                .then_inc(part_ready, 1)
            dve.wait_ge(mean_done, 1)
            for i in range(2):
                dve.tensor_tensor(quad(xc, i), quad(x_sb, i), stat[:, 0:N].unsqueeze(1).to_broadcast([P, KG, N]),
                                  ALU.subtract).then_inc(centered, 1)
            dve.wait_ge(rows_landed, 16)
            dve.tensor_copy(erow_b, erow).then_inc(rows_ready, 1)
            dve.wait_ge(squared, 1)
            dve.tensor_reduce(part[:, 1], sq[:, :, :].rearrange("p t n -> p n t"), axis=AX_X, op=ALU.add)\
                .then_inc(sq_ready, 1)
            dve.wait_ge(edges_landed, 16)
            then(dve.tensor_copy(ecol_f[:, :, :], ecol[:, :, :]))
            then(dve.tensor_scalar(code[:, :], ecol_f[:, 2, :], 0.0, float(TYPES), ALU.is_equal, ALU.mult))
            dve.tensor_tensor(code[:, :], code[:, :], ecol_f[:, 2, :], ALU.add).then_inc(codes_ready, 1)
            then(dve.scalar_tensor_tensor(key_col[:, :], ecol_f[:, 0, :], float(N), ecol_f[:, 1, :],
                                          ALU.mult, ALU.add))
            then(dve.memset(dup[:, :, :], 0.0))
            dve.wait_ge(var_done, 1)
            dve.tensor_scalar(rscr_n[:, 0:1], stat[0:N, 128:129], EPS, None, ALU.add).then_inc(var_out, 1)
            dve.wait_ge(rstd_n_ready, 1)
            dve.tensor_scalar(rdiag[:, :], ident[0:N, 0:N], rstd_n[:, 0:1], None, ALU.mult).then_inc(rdiag_ready, 1)
            dve.wait_ge(rstd_done, 1)
            then(dve.tensor_copy(rstd[:, :], stat[:, 256:256 + N]))
            dve.wait_ge(cols_landed, 16)

            def evacuate(c):
                m, p = c // CPM, c % CPM
                dve.wait_ge(chunk_done, c + 1)
                if m in (WQ, WK, WV):
                    to = {WQ: q, WK: k, WV: v}[m]
                    b = {WQ: 0, WK: 1, WV: 4}[m]
                    then(dve.tensor_tensor(half(to, p), pair(c), rstd_pair, ALU.mult))
                    dve.tensor_tensor(half(to, p), half(to, p), biases(b, p), ALU.add).then_inc(evac, 1)
                else:
                    to = {WIQ: q2, WIK: k2}[m]
                    b = {WIQ: 2, WIK: 3}[m]
                    dve.tensor_tensor(half(to, p), pair(c), biases(b, p), ALU.add).then_inc(evac, 1)

            def count_later(c):
                if c < EC - 1:
                    dve.tensor_scalar(same[:, P * (c + 1):], keys[:, P * (c + 1):], key_col[:, c:c + 1], 0.0,
                                      ALU.is_equal, ALU.add, accum_out=dup[:, 0, c:c + 1])
                then(dve.scalar_tensor_tensor(same[:, P * c:P * (c + 1)], keys[:, P * c:P * (c + 1)],
                                              key_col[:, c:c + 1], later[:, :], ALU.is_equal, ALU.mult,
                                              accum_out=dup[:, 1, c:c + 1]))

            def one_hot_sources():
                then(dve.tensor_tensor(dup[:, 0], dup[:, 0], dup[:, 1], ALU.add))
                then(dve.scalar_tensor_tensor(dup[:, 1], dup[:, 0], float(P), ecol_f[:, 0, :], ALU.mult, ALU.add))
                dve.tensor_tensor(src_hot[:, :, :], iota_f[:, :].unsqueeze(1).to_broadcast([P, EC, N]),
                                  dup[:, 1, :].unsqueeze(2).to_broadcast([P, EC, N]), ALU.is_equal)\
                    .then_inc(src_ready, 1)

            def build_mask():
                dve.wait_ge(tw_ready, 1)
                then(dve.scalar_tensor_tensor(tw[:, 1, :], tw[:, 0, :], 0.0, tw[:, 3, :], ALU.max, ALU.add))
                dve.wait_ge(cells_done, 1)
                then(dve.scalar_tensor_tensor(cell_t[:, :], aux[3][0:N, 0:N], 0.0, ident[0:N, 0:N],
                                              ALU.is_equal, ALU.mult))
                then(dve.scalar_tensor_tensor(cell[:, :], cell_t[:, :], float(TYPES), aux[3][0:N, 0:N],
                                              ALU.mult, ALU.add))
                then(dve.tensor_scalar(mask[:, :], cell[:, :], 0.0, ABSENT, ALU.is_equal, ALU.mult))
                for t in range(TYPES):
                    then(dve.tensor_scalar(cell_t[:, :], cell[:, :], float(t + 1), tw[:, 1, t:t + 1],
                                           ALU.is_equal, ALU.mult))
                    then(dve.tensor_tensor(mask[:, :], mask[:, :], cell_t[:, :], ALU.add))

            def scores(g):
                dve.wait_ge(scores_done, g // 2 + 1)
                s = prob[0:N, g]
                dve.scalar_tensor_tensor(s, aux[g][0:N, 0:4 * N].rearrange("p (h n) -> p h n", h=4), SCALE,
                                         mask[:, :].unsqueeze(1).to_broadcast([N, 4, N]), ALU.mult, ALU.add)\
                    .then_inc(scores_out, 1)
                dve.wait_ge(scores_out, g + 1)
                then(dve.tensor_reduce(smax[:, g], s, axis=AX_X, op=ALU.max))
                dve.tensor_tensor(s, s, smax[:, g].unsqueeze(2).to_broadcast([N, 4, N]), ALU.subtract)\
                    .then_inc(prob_ready, 1)

            def normalise(g):
                dve.wait_ge(exped, g + 1)
                s = prob[0:N, g]
                then(dve.tensor_reduce(ssum[:, g], s, axis=AX_X, op=ALU.add))
                then(dve.reciprocal(sinv[:, g], ssum[:, g]))
                dve.tensor_tensor(s, s, sinv[:, g].unsqueeze(2).to_broadcast([N, 4, N]), ALU.mult)\
                    .then_inc(prob_normed, 1)

            def split_lo(c):
                dve.wait_ge(hi_done, c - FIRST_SPLIT + 1)
                dve.tensor_tensor(w_lo[:, c % PARTS], ring[:, c % RING], w_hi[:, c % PARTS].bitcast(F32),
                                  ALU.subtract).then_inc(lo_done, 1)

            for c in range(CPM * WV):
                evacuate(c)
                if 2 <= c <= 7:
                    if c == 2:
                        dve.wait_ge(keys_out, 3)
                        dve.wait_ge(const_done, 7)
                    count_later(2 * c - 4)
                    count_later(2 * c - 3)
                if c == 8:
                    one_hot_sources()
                if c == 12:
                    build_mask()
            evacuate(16)
            scores(0)
            scores(1)
            evacuate(17)
            normalise(0)
            scores(2)
            evacuate(18)
            normalise(1)
            scores(3)
            evacuate(19)
            split_lo(22)
            dve.wait_ge(v_hi, 1)
            dve.tensor_tensor(quad(a_lo, 1), quad(v, 1), quad(a_hi, 1).bitcast(F32), ALU.subtract).then_inc(v_lo, 1)
            normalise(2)
            normalise(3)
            for c in range(23, 27):
                split_lo(c)
            for i in range(2):
                dve.wait_ge(heads_done, i + 1)
                dve.tensor_tensor(quad(ao, i), quad_psum(aux[i]),
                                  bias[:, 5, KG * i:KG * (i + 1)].unsqueeze(2).to_broadcast([P, KG, N]), ALU.add)\
                    .then_inc(ao_ready, 1)
                dve.wait_ge(ao_ready, i + 1)
                dve.wait_ge(ao_hi, i + 1)
                dve.tensor_tensor(quad(a_lo, i), quad(ao, i), quad(a_hi, i).bitcast(F32), ALU.subtract)\
                    .then_inc(ao_lo, 1)
            for c in range(27, 31):
                split_lo(c)
            for i in range(2):
                if i == 0:
                    dve.wait_ge(xb_ready, 1)
                dve.wait_ge(chunk_done, 27 + i)
                dve.tensor_tensor(cut(x1, i), nat_bank[WO, i][0:N, :], cut(x1, i), ALU.add).then_inc(x1_ready, 1)
                dve.wait_ge(x1_ready, i + 1)
                then(dve.bn_stats(stats[:, i, :], cut(x1, i)))
            then(dve.bn_aggr(moments[:, :], stats[:, :, :]))
            dve.tensor_scalar(rscr_n[:, 1:2], moments[:, 1:2], EPS, None, ALU.add).then_inc(var_out, 1)
            dve.wait_ge(rstd_n_ready, 2)
            for i in range(2):
                dve.tensor_scalar(cut(hid, i), cut(x1, i), moments[:, 0:1], rstd_n[:, 1:2], ALU.subtract, ALU.mult)\
                    .then_inc(normed, 1)
            for i in range(2):
                dve.wait_ge(xn_hi, i + 1)
                dve.tensor_tensor(quad(a_lo, i), quad_psum(aux[i]), quad(a_hi, i).bitcast(F32), ALU.subtract)\
                    .then_inc(xn_lo, 1)
            split_lo(31)
            split_lo(32)
            split_lo(33)
            dve.wait_ge(logits_done, 1)
            dve.wait_ge(small_landed, 48)
            then(dve.tensor_tensor(logit[:, :], aux[2][0:N, 0:EXPERTS], br_sb[:, :], ALU.add))
            then(dve.max(top[:, :], logit[:, :]))
            dve.tensor_scalar(ntop[:, :], top[:, 0:1], -1.0, None, ALU.mult).then_inc(logits_ready, 1)
            dve.wait_ge(gate_exped, 1)
            then(dve.scalar_tensor_tensor(gate[:, :], logit[:, :], top[:, 1:2], gate[:, :], ALU.is_ge, ALU.mult))
            then(dve.tensor_reduce(gsum[:, 0:1], gate[:, :], axis=AX_X, op=ALU.add))
            then(dve.reciprocal(gsum[:, 1:2], gsum[:, 0:1]))
            dve.tensor_scalar(gate[:, :], gate[:, :], gsum[:, 1:2], None, ALU.mult).then_inc(gate_ready, 1)
            dve.wait_ge(gateT_done, 1)
            dve.tensor_copy(gateT[:, :], aux[3][0:EXPERTS, 0:N]).then_inc(gateT_out, 1)

            def hidden(i):
                dve.wait_ge(chunk_done, 31 + i)
                dve.tensor_tensor(cut(hid, i), nat_bank[W1, i][0:N, :], cut(b1_sb, i), ALU.add).then_inc(hid_ready, 1)

            def weigh(i):
                dve.wait_ge(gelu_done, i + 1)
                dve.tensor_tensor(cut(hid, i).rearrange("p (e j) -> p e j", e=4),
                                  cut(hid, i).rearrange("p (e j) -> p e j", e=4),
                                  gate[:, 4 * i:4 * i + 4].unsqueeze(2).to_broadcast([N, 4, P]), ALU.mult)\
                    .then_inc(weighed, 1)

            def hidden_lo(i):
                dve.wait_ge(hid_hi, i + 1)
                dve.tensor_tensor(quad(g_lo, i), quad_psum(aux[i]), quad(g_hi, i).bitcast(F32), ALU.subtract)\
                    .then_inc(hid_lo, 1)

            hidden(0)
            weigh(0)
            split_lo(34)
            hidden_lo(0)
            hidden(1)
            weigh(1)
            hidden_lo(1)
            split_lo(35)
            for i in range(3):
                dve.wait_ge(chunk_done, 35 + (i > 0))
                lo, hi = (0, HALF, 3 * HALF // 2, D)[i:i + 2]
                h = int(i > 0)
                dve.tensor_tensor(res[:, lo:hi], nat_bank[W2, h][0:N, lo - HALF * h:hi - HALF * h], x1[:, lo:hi], ALU.add)\
                    .then_inc(res_ready, 1)

        @block.tensor
        def _(pe):
            def stationary_chunk(c, rhs, ready):
                pe.wait_ge(w_landed[c % RING], 16 * (c // RING + 1))
                if c >= ACC:
                    pe.wait_ge(evac, c - ACC + 1)
                w = ring[:, c % RING].rearrange("p a b -> p (a b)").rearrange("p (t k j) -> p t k j", t=PER, k=KT)
                for t in range(PER):
                    for kt in range(KT):
                        if t == 0:
                            ready(kt)
                        last = nc.tensor.matmul(acc[c % ACC][:, N * t:N * (t + 1)], w[:, t, kt],
                                                rhs[:, kt], start=(kt == 0), stop=(kt == KT - 1))
                last.then_inc(chunk_done, 1)

            def matrix(m, rhs, made_by):
                def ready(kt):
                    if c == CPM * m and kt % PER == 0:
                        pe.wait_ge(evac, CPM * made_by + kt // PER + 1)
                for c in range(CPM * m, CPM * (m + 1)):
                    stationary_chunk(c, rhs, ready)

            def nothing(kt):
                pass

            def moving_chunk(c, lhsT, fresh=True):
                m, kg, h = chunk_of(c)
                pe.wait_ge(w_landed[c % RING], 16 * (c // RING + 1))
                for i in range(KG):
                    last = nc.tensor.matmul(nat_bank[m, h][0:N, :], lhsT[:, KG * kg + i], ring[:, c % RING, i],
                                            start=(kg == 0 and i == 0), stop=(kg == 1 and i == KG - 1))
                last.then_inc(chunk_done, 1)

            def split_chunk(c, hi, lo, fresh=True):
                m, kg, h = chunk_of(c)
                pe.wait_ge(lo_done, c - FIRST_SPLIT + 1)
                out_ = nat_bank[m, h][0:N, :]
                for i in range(KG):
                    kt = KG * kg + i
                    nc.tensor.matmul(out_, hi[:, kt], w_hi[:, c % PARTS, i], start=(fresh and kg == 0 and i == 0),
                                     stop=False)
                    nc.tensor.matmul(out_, hi[:, kt], w_lo[:, c % PARTS, i], start=False, stop=False)
                    last = nc.tensor.matmul(out_, lo[:, kt], w_hi[:, c % PARTS, i], start=False,
                                            stop=(kg == 1 and i == KG - 1))
                last.then_inc(chunk_done, 1)

            pe.wait_ge(warm_ready, 1)
            for i in range(WARM):
                nc.tensor.matmul(acc[ACC - 1][:, :], warm[:, 0:P], warm[:, :], start=True, stop=True)
            pe.wait_ge(const_done, 7)
            pe.wait_ge(part_ready, 1)
            nc.tensor.matmul(stat[:, 0:N], mean_w[:, :], part[:, 0], start=True, stop=True).then_inc(mean_done, 1)
            for i in range(WARM_2):
                nc.tensor.matmul(acc[ACC - 1][:, :], warm[:, 0:P], warm[:, :], start=True, stop=True)

            def ready_centered(kt):
                if kt % 4 == 0:
                    pe.wait_ge(centered, kt // 4 + 1)

            stationary_chunk(0, xc, ready_centered)
            pe.wait_ge(sq_ready, 1)
            nc.tensor.matmul(stat[0:N, 128:129], part[:, 1], mean_w[:, 0:1], start=True, stop=True).then_inc(var_done, 1)
            stationary_chunk(1, xc, nothing)
            pe.wait_ge(rdiag_ready, 1)
            nc.tensor.matmul(stat[:, 256:256 + N], ones[:, :], rdiag[:, :], start=True, stop=True).then_inc(rstd_done, 1)
            pe.wait_ge(rows_ready, 1)
            for i in range(3):
                nc.tensor.matmul(aux[i][:, :], key_w[:, :], erow_b[:, 512 * i:512 * (i + 1)],
                                 start=True, stop=True).then_inc(keys_done, 1)
            for c in range(2, CPM * 2):
                stationary_chunk(c, xc, nothing)
            matrix(WIQ, q, WQ)
            pe.wait_ge(src_ready, 1)
            pe.wait_ge(dst_ready, 1)
            for c in range(EC):
                last = nc.tensor.matmul(aux[3][0:N, 0:N], src_hot[:, c], dst_hot[:, c],
                                        start=(c == 0), stop=(c == EC - 1))
            last.then_inc(cells_done, 1)
            matrix(WIK, k, WK)
            stationary_chunk(16, xc, nothing)
            pe.wait_ge(evac, CPM * (WIK + 1))
            for h in range(HEADS):
                g, i, s = 2 * (h // 8) + h % 2, (h % 8) // 2, HD * (h % 2)
                last = nc.tensor.matmul(aux[g][0:N, N * i:N * (i + 1)], q2[s:s + HD, h // 2], k2[s:s + HD, h // 2],
                                        start=True, stop=True)
                if h % 8 == 7:
                    last.then_inc(scores_done, 1)
            for c in range(17, 20):
                stationary_chunk(c, xc, nothing)

            pe.wait_ge(evac, 20)
            moving_chunk(20, v)
            moving_chunk(21, v)
            pe.wait_ge(v_lo, 1)
            split_chunk(22, a_hi, a_lo)
            for g in range(4):
                pe.wait_ge(prob_normed, g + 1)
                for i in range(4):
                    last = nc.tensor.transpose(aux[g][0:N, N * i:N * (i + 1)], prob[0:N, g, i], ident[0:N, 0:N])
                last.then_inc(probT_done, 1)
            split_chunk(23, a_hi, a_lo)
            for i in range(2):
                pe.wait_ge(v2n_out, i + 1)
                pe.wait_ge(probT_out, 4)
                for t in range(4):
                    for s in range(2):
                        h = 2 * (4 * i + t) + s
                        g, j = 2 * (h // 8) + h % 2, (h % 8) // 2
                        last = nc.tensor.matmul(aux[i][HD * s:HD * (s + 1), N * t:N * (t + 1)], v2n[:, h],
                                                probT[0:N, g, j], start=True, stop=True)
                last.then_inc(heads_done, 1)
            for c in range(24, 28):
                if c in (24, 26):
                    pe.wait_ge(ao_lo, (c - 24) // 2 + 1)
                split_chunk(c, a_hi, a_lo)
            for i in range(2):
                pe.wait_ge(normed, i + 1)
                for t in range(KG):
                    kt = KG * i + t
                    last = nc.tensor.transpose(aux[i][:, N * t:N * (t + 1)], hid[:, P * kt:P * (kt + 1)], ident[0:N, 0:N])
                last.then_inc(xnT_done, 1)
            for c in range(28, 30):
                pe.wait_ge(xn_lo, 1)
                split_chunk(c, a_hi, a_lo)
            pe.wait_ge(xnT_out, 2)
            for kt in range(KT):
                last = nc.tensor.matmul(aux[2][0:N, 0:EXPERTS], xnT[:, kt], wr[:, kt], start=(kt == 0), stop=(kt == KT - 1))
            last.then_inc(logits_done, 1)
            pe.wait_ge(xn_lo, 2)
            split_chunk(30, a_hi, a_lo)
            split_chunk(31, a_hi, a_lo)
            pe.wait_ge(gate_ready, 1)
            nc.tensor.transpose(aux[3][0:EXPERTS, 0:N], gate[:, :], ident[0:N, 0:N]).then_inc(gateT_done, 1)
            pe.wait_ge(gateT_out, 1)
            pe.wait_ge(b2_landed, 16)
            for h in range(2):
                nc.tensor.matmul(nat_bank[W2, h][0:N, :], gateT[:, :], cut(b2_sb, h), start=True, stop=False)

            def hidden_transposed(i):
                pe.wait_ge(weighed, i + 1)
                for t in range(KG):
                    kt = KG * i + t
                    last = nc.tensor.transpose(aux[i][:, N * t:N * (t + 1)], hid[:, P * kt:P * (kt + 1)], ident[0:N, 0:N])
                last.then_inc(hidT_done, 1)

            hidden_transposed(0)
            pe.wait_ge(hid_lo, 1)
            split_chunk(32, g_hi, g_lo, fresh=False)
            hidden_transposed(1)
            split_chunk(33, g_hi, g_lo, fresh=False)
            pe.wait_ge(hid_lo, 2)
            split_chunk(34, g_hi, g_lo, fresh=False)
            split_chunk(35, g_hi, g_lo, fresh=False)


def kernel(x, src, dst, edge_type_5, L0_gnn_edge_type_weights, L0_gnn_wq, L0_gnn_bq, L0_gnn_wk, L0_gnn_bk, L0_gnn_wv,
           L0_gnn_bv, L0_gnn_wiq, L0_gnn_biq, L0_gnn_wik, L0_gnn_bik, L0_gnn_wiv, L0_gnn_biv, L0_gnn_wo, L0_gnn_bo,
           L0_ffn_W1, L0_ffn_b1, L0_ffn_W2, L0_ffn_b2, L0_ffn_Wr, L0_ffn_br):
    import numpy as np
    import concourse.bacc as bacc
    from concourse.bass_utils import run_bass_kernel_spmd

    a = np.asarray

    def stationary(w_out_in):
        return a(w_out_in).reshape(CPM, PER, P, KT, P).transpose(0, 4, 1, 3, 2).reshape(CPM, P, KG, HALF)

    def moving(w_in_out):
        return w_in_out.reshape(2, KG, P, 2, HALF).transpose(0, 3, 2, 1, 4).reshape(CPM, P, KG, HALF)

    mats = [stationary(w) for w in (L0_gnn_wq, L0_gnn_wk, L0_gnn_wiq, L0_gnn_wik, L0_gnn_wv)]
    mats += [moving(w) for w in (a(L0_gnn_wiv).T, a(L0_gnn_wo).T, a(L0_ffn_W1).transpose(1, 0, 2), a(L0_ffn_W2))]
    biases = np.stack([a(b).reshape(8, P) for b in (L0_gnn_bq, L0_gnn_bk, L0_gnn_biq, L0_gnn_bik, L0_gnn_bv,
                                                    L0_gnn_biv)])
    router = a(L0_ffn_Wr).reshape(KT, P, EXPERTS)
    edges = np.stack([a(e) for e in (src, dst, edge_type_5)])
    arrays = {
        "xT": np.ascontiguousarray(a(x).T.reshape(KT, P, N).transpose(1, 0, 2)),
        "x": a(x),
        "weights": np.ascontiguousarray(np.concatenate(mats)),
        "cols": np.ascontiguousarray(np.concatenate([biases.transpose(2, 0, 1), router.transpose(1, 0, 2)], axis=1)),
        "edge_cols": np.ascontiguousarray(edges.reshape(3, EC, P).transpose(2, 0, 1)),
        "edge_rows": np.ascontiguousarray(edges[0:2]),
        "type_weights": a(L0_gnn_edge_type_weights).reshape(1, TYPES),
        "bo": a(L0_gnn_bo).reshape(1, D),
        "b1": a(L0_ffn_b1).reshape(1, D),
        "br": a(L0_ffn_br).reshape(1, EXPERTS),
        "b2": a(L0_ffn_b2),
    }
    nc = bacc.Bacc("TRN2", target_bir_lowering=False, num_devices=1)
    args = [nc.dram_tensor(n, v.shape, mybir.dt.from_np(v.dtype), kind="ExternalInput").ap() for n, v in arrays.items()]
    args.append(nc.dram_tensor("out", (N, D), F32, kind="ExternalOutput").ap())
    gnn_ffn_kernel(nc, *args)
    r = run_bass_kernel_spmd(nc, [arrays], core_ids=[0])
    return r.results[0]["out"]
```

```python
from contextlib import ExitStack

import concourse.bass as bass
from concourse import mybir

ALU = mybir.AluOpType
ACT = mybir.ActivationFunctionType
F32 = mybir.dt.float32
F32R = mybir.dt.float32r
BF16 = mybir.dt.bfloat16
I32 = mybir.dt.int32
AX_X = mybir.AxisListType.X

P = 128
N = 96
D = 1024
KT = D // P
HEADS = 16
HD = D // HEADS
EDGES = 1536
EC = EDGES // P
EXPERTS = 8
TYPES = 4
EPS = 1e-5
SCALE = 1.0 / HD ** 0.5
ABSENT = -1.0e30

WQ, WK, WIQ, WIK, WV, WIV, WO, W1, W2 = range(9)
MATS = 9
STATIONARY = (WQ, WIQ, WIK)
HALF_FIRST = (WK, WV, WIV, W1)
PER = 2
HALF = D // 2
KG = KT // 2
CPM = 4
CHUNKS = MATS * CPM
ORDER = [(WQ, i) for i in range(CPM)]
ORDER += [(WK, 0), (WIQ, 0), (WK, 1), (WK, 2), (WIQ, 1), (WK, 3), (WV, 0), (WIK, 0)]
ORDER += [(WV, 1), (WIK, 1), (WIQ, 2), (WV, 2), (WIQ, 3), (WIK, 2), (WV, 3), (WIK, 3)]
ORDER += [(m, i) for m in (WIV, WO, W1, W2) for i in range(CPM)]
WHOLE = [c for c in range(CHUNKS) if ORDER[c][0] in STATIONARY]
SPLIT = [c for c in range(CHUNKS) if ORDER[c][0] not in STATIONARY]
EARLY = (4, 6, 7, 9, 10, 12, 34, 35)
DIGIT = 16
OUT_PARTS = ((0, HALF), (HALF, 3 * HALF // 2), (3 * HALF // 2, D))
RING = 8
PARTS = 5
WARM = 8
WARM_2 = 4
WARM_LN = 10
WARM_XN = 4
ACC = 3


def gnn_ffn_kernel(nc, xT, x, weights, cols, edge_cols, edge_rows, type_weights, bo, b1, br, b2, out):
    ctx = ExitStack()
    with ctx:
        def sb(name, shape, dt=F32):
            return ctx.enter_context(nc.sbuf_tensor(name, shape, dt))

        def bank(name):
            return ctx.enter_context(nc.psum_tensor(name, [P, 512], F32))

        def sem(name):
            return ctx.enter_context(nc.semaphore(name))

        ring = sb("ring", [P, RING, KG, HALF])
        w_hi = sb("w_hi", [P, PARTS, KG, HALF], F32R)
        w_lo = sb("w_lo", [P, PARTS, KG, HALF], F32R)
        xc = sb("xc", [P, KT, N])
        q = sb("q", [P, KT, N])
        k = sb("k", [P, KT, N])
        q2 = sb("q2", [P, KT, N])
        k2 = sb("k2", [P, KT, N])
        x_sb, sq = q2, k2
        v = xc
        ao = k
        xnT = q
        a_hi = sb("a_hi", [P, KT, N], F32R)
        a_lo = sb("a_lo", [P, KT, N], F32R)
        g_hi = sb("g_hi", [P, KT, N], F32R)
        g_lo = sb("g_lo", [P, KT, N], F32R)
        v2n = sb("v2n", [N, HEADS, HD])
        nat = v2n[:, :, :].rearrange("p h d -> p (h d)")
        prob = sb("prob", [P, 4, 4, N])
        probT = sb("probT", [P, 4, 4, N])
        x1_all = sb("x1_all", [P, D])
        x1 = x1_all[0:N, :]
        hid_all = sb("hid_all", [P, D])
        hid = hid_all[0:N, :]
        res = v2n[:, :, :].rearrange("p h d -> p (h d)")
        x1_sq = [t[0:N, :, :].rearrange("p t n -> p (t n)")[:, 0:HALF] for t in (q2, k2)]
        b1_all = sb("b1_all", [P, D])
        b1_sb = b1_all[0:N, :]
        x1_sum = sb("x1_sum", [N, 2])
        x1_mean = sb("x1_mean", [N, 1])
        x1_var = sb("x1_var", [N, 2])
        part = sb("part", [P, 2, N])
        rstd = sb("rstd", [P, N])
        rscr_n = sb("rscr_n", [N, 2])
        rstd_n = sb("rstd_n", [N, 2])
        rdiag = sb("rdiag", [N, N])
        cols_sb = sb("cols_sb", [P, 6 + EXPERTS, 8])
        bias = cols_sb[:, 0:6, :]
        wr = cols_sb[:, 6:14, :]
        b2_sb = prob[0:EXPERTS, :, :, :].rearrange("p g h n -> p (g h n)")[:, 0:D]
        br_sb = sb("br_sb", [N, EXPERTS])
        ident = sb("ident", [P, P])
        mean_w = sb("mean_w", [P, P])
        ones = sb("ones", [N, P])
        mhalf = sb("mhalf", [N, 1])
        ecol = sb("ecol", [P, 3, EC], I32)
        ecol_f = sb("ecol_f", [P, 3, EC])
        erow = probT[0:2, :, :, :].rearrange("p g h n -> p (g h n)").bitcast(I32)
        erow_b = v2n[0:2, :, :].rearrange("p h d -> p (h d)").bitcast(BF16)[:, 0:EDGES]
        key_w = sb("key_w", [2, P], BF16)
        key_w_i = sb("key_w_i", [2, P], I32)
        keys = prob[:, :, :, :].rearrange("p g h n -> p (g h n)")
        key_col = sb("key_col", [P, EC])
        weight_of_col = sb("weight_of_col", [P, EC])
        later = x1_all[:, 0:P]
        same = k2[:, :, :].rearrange("p t n -> p (t n)").bitcast(BF16)
        dup = sb("dup", [P, 2, EC])
        code = sb("code", [P, EC])
        iota_i = x1_all[:, P:P + N].bitcast(I32)
        iota_f = x1_all[:, P + N:P + 2 * N]
        src_hot = same[:, 0:EC * N].rearrange("p (c n) -> p c n", c=EC)
        dst_hot = hid_all[:, :].bitcast(BF16)[:, 0:EC * N].rearrange("p (c n) -> p c n", c=EC)
        cell = sb("cell", [N, N])
        digit_i = sb("digit_i", [N, N], I32)
        cell_t = sb("cell_t", [N, N])
        mask = sb("mask", [N, N])
        tw = sb("tw", [N, 4, TYPES])
        smax = sb("smax", [N, 4, 4])
        ssum = sb("ssum", [N, 4, 4])
        sinv = sb("sinv", [N, 4, 4])
        logit = sb("logit", [N, EXPERTS])
        top = sb("top", [N, 8])
        ntop = sb("ntop", [N, 1])
        gate = sb("gate", [N, EXPERTS])
        gsum = sb("gsum", [N, 2])
        gateT = sb("gateT", [EXPERTS, N])

        warm = b1_all[:, 0:256].bitcast(BF16)

        acc = [bank(f"acc{i}") for i in range(ACC)]
        aux = [bank(f"aux{i}") for i in range(4)]
        stat = bank("stat")

        w_landed = [sem(f"w_landed{i}") for i in range(RING)]
        x_landed = sem("x_landed")
        xn_landed = sem("xn_landed")
        cols_landed = sem("cols_landed")
        edges_landed = sem("edges_landed")
        rows_landed = sem("rows_landed")
        small_landed = sem("small_landed")
        b2_landed = sem("b2_landed")
        const_done = sem("const_done")
        warm_ready = sem("warm_ready")
        chunk_done = sem("chunk_done")
        evac = sem("evac")
        hi_done = sem("hi_done")
        lo_done = sem("lo_done")
        early_hi = sem("early_hi")
        early_lo = sem("early_lo")
        part_ready = sem("part_ready")
        mean_done = sem("mean_done")
        centered = sem("centered")
        squared = sem("squared")
        sq_ready = sem("sq_ready")
        var_done = sem("var_done")
        var_out = sem("var_out")
        rstd_n_ready = sem("rstd_n_ready")
        rdiag_ready = sem("rdiag_ready")
        rstd_done = sem("rstd_done")
        xb_ready = sem("xb_ready")
        step = sem("step")
        pool_step = sem("pool_step")
        act_step = sem("act_step")
        rows_ready = sem("rows_ready")
        keys_done = sem("keys_done")
        keys_out = sem("keys_out")
        codes_ready = sem("codes_ready")
        src_ready = sem("src_ready")
        dst_ready = sem("dst_ready")
        cells_done = sem("cells_done")
        tw_ready = sem("tw_ready")
        scores_done = sem("scores_done")
        scores_out = sem("scores_out")
        prob_ready = sem("prob_ready")
        exped = sem("exped")
        prob_normed = sem("prob_normed")
        probT_done = sem("probT_done")
        probT_out = sem("probT_out")
        xc_hi = sem("xc_hi")
        xc_lo = sem("xc_lo")
        k_nat = sem("k_nat")
        kT_done = sem("kT_done")
        k_ready = sem("k_ready")
        v_nat = sem("v_nat")
        vT_done = sem("vT_done")
        v_ready = sem("v_ready")
        v_hi = sem("v_hi")
        v_lo = sem("v_lo")
        v2n_out = sem("v2n_out")
        heads_done = sem("heads_done")
        ao_ready = sem("ao_ready")
        ao_hi = sem("ao_hi")
        ao_lo = sem("ao_lo")
        x1_ready = sem("x1_ready")
        x1_centered = sem("x1_centered")
        x1_squared = sem("x1_squared")
        xnT_done = sem("xnT_done")
        xn_hi = sem("xn_hi")
        xnT_out = sem("xnT_out")
        xn_lo = sem("xn_lo")
        logits_done = sem("logits_done")
        logits_ready = sem("logits_ready")
        gate_exped = sem("gate_exped")
        gate_ready = sem("gate_ready")
        gateT_done = sem("gateT_done")
        gateT_out = sem("gateT_out")
        hid_ready = sem("hid_ready")
        gelu_done = sem("gelu_done")
        weighed = sem("weighed")
        hidT_done = sem("hidT_done")
        hid_hi = sem("hid_hi")
        hid_lo = sem("hid_lo")
        res_ready = sem("res_ready")
        stored = sem("stored")

        block = ctx.enter_context(nc.Block())

        def pair_of(t, p):
            return t[:, PER * p:PER * (p + 1), :]

        def quad(t, i):
            return t[:, KG * i:KG * (i + 1), :]

        def pair_psum(b):
            return b[:, 0:PER * N].rearrange("p (t n) -> p t n", t=PER)

        def cut(t, i):
            return t[:, HALF * i:HALF * (i + 1)]

        def quad_psum(b):
            return b[:, 0:KG * N].rearrange("p (t n) -> p t n", t=KG)

        nat_bank = {(WK, 0): stat, (WK, 1): aux[3], (WV, 0): stat, (WV, 1): stat, (WIV, 0): acc[0],
                    (WIV, 1): acc[1], (WO, 0): acc[2], (WO, 1): stat, (W1, 0): acc[0], (W1, 1): acc[1],
                    (W2, 0): acc[2], (W2, 1): stat}

        W2_QUARTERS = ((stat, 0, HALF // 2), (acc[0], HALF // 2, HALF))

        def chunk_of(c):
            m, i = ORDER[c]
            return (m, i % 2, i // 2) if m in HALF_FIRST else (m, i // 2, i % 2)

        def parts_of(c):
            return SPLIT.index(c) % PARTS

        def acc_of(c):
            return acc[WHOLE.index(c) % ACC]

        def landed(engine, c):
            engine.wait_ge(w_landed[c % RING], 16 * (c // RING + 1))

        @block.sync
        def _(sp):
            sp.dma_start(x_sb[:, :, :], xT).then_inc(x_landed, 16)
            for c in range(CHUNKS):
                if c >= RING:
                    old = c - RING
                    if old in SPLIT:
                        sp.wait_ge(lo_done, SPLIT.index(old) + 1)
                    else:
                        sp.wait_ge(chunk_done, old + 1)
                sp.dma_start(ring[:, c % RING], weights[c]).then_inc(w_landed[c % RING], 16)
            for i, (lo, hi) in enumerate(OUT_PARTS):
                sp.wait_ge(res_ready, i + 1)
                sp.dma_start(out[:, lo:hi], res[:, lo:hi]).then_inc(stored, 16)
            sp.wait_ge(stored, 16 * len(OUT_PARTS))

        @block.gpsimd
        def _(pool):
            pool.memset(warm[:, :], 0.0).then_inc(warm_ready, 1)
            pool.memset(mean_w[:, :], 1.0 / D).then_inc(const_done, 1)
            pool.memset(ones[:, :], 1.0).then_inc(const_done, 1)
            pool.memset(mhalf[:, :], -0.5).then_inc(const_done, 1)
            for c in range(EC):
                last = pool.memset(weight_of_col[:, c:c + 1], 2.0 * DIGIT ** c)
            last.then_inc(const_done, 1)
            pool.memset(ident[:, :], 0.0).then_inc(pool_step, 1)
            pool.memset(later[:, :], 1.0).then_inc(pool_step, 1)
            pool.wait_ge(pool_step, 2)
            pool.affine_select(out=ident[:, :], in_=ident[:, :], compare_op=ALU.not_equal, fill=1.0, base=0,
                               pattern=[[-1, P]], channel_multiplier=1).then_inc(const_done, 1)
            pool.affine_select(out=later[:, :], in_=later[:, :], compare_op=ALU.is_gt, fill=0.0, base=0,
                               pattern=[[1, P]], channel_multiplier=-1).then_inc(const_done, 1)
            pool.iota(iota_i[:, :], pattern=[[1, N]], base=0, channel_multiplier=0).then_inc(pool_step, 1)
            pool.iota(key_w_i[:, :], pattern=[[0, P]], base=N, channel_multiplier=1 - N).then_inc(pool_step, 1)
            pool.wait_ge(pool_step, 4)
            pool.tensor_copy(key_w[:, :], key_w_i[:, :]).then_inc(const_done, 1)
            pool.tensor_copy(iota_f[:, :], iota_i[:, :]).then_inc(const_done, 1)
            pool.wait_ge(const_done, 8)
            pool.wait_ge(var_out, 1)
            pool.tensor_tensor(rstd_n[:, 0:1], rscr_n[:, 0:1], mhalf[:, :], ALU.pow).then_inc(rstd_n_ready, 1)
            pool.wait_ge(codes_ready, 1)
            for c in range(EC):
                last = pool.tensor_scalar(dst_hot[:, c], iota_f[:, :], ecol_f[:, 1, c:c + 1], code[:, c:c + 1],
                                          ALU.is_equal, ALU.mult)
            last.then_inc(dst_ready, 1)
            pool.wait_ge(xn_landed, 32)
            pool.tensor_tensor(x1[:, :], x1[:, :], hid[:, :], ALU.add).then_inc(xb_ready, 1)
            pool.wait_ge(var_out, 2)
            pool.tensor_tensor(rstd_n[:, 1:2], rscr_n[:, 1:2], mhalf[:, :], ALU.pow).then_inc(rstd_n_ready, 1)

        @block.scalar
        def _(act):
            act.dma_start(cols_sb[:, :, :], cols).then_inc(cols_landed, 16)
            act.dma_start(ecol[:, :, :], edge_cols).then_inc(edges_landed, 16)
            act.dma_start(erow[:, :], edge_rows).then_inc(rows_landed, 16)
            act.dma_start(tw[:, 0, :], type_weights.to_broadcast([N, TYPES])).then_inc(small_landed, 16)
            act.dma_start(br_sb[:, :], br.to_broadcast([N, EXPERTS])).then_inc(small_landed, 16)
            act.wait_ge(centered, 2)
            act.activation(sq[:, :, :], xc[:, :, :], ACT.Square).then_inc(squared, 1)
            act.copy(g_hi[:, :, :], xc[:, :, :]).then_inc(xc_hi, 1)
            for i in range(3):
                act.wait_ge(keys_done, i + 1)
                act.copy(keys[:, 512 * i:512 * (i + 1)], aux[i][:, :]).then_inc(keys_out, 1)

            def split_hi(c):
                landed(act, c)
                if SPLIT.index(c) >= PARTS:
                    act.wait_ge(chunk_done, SPLIT[SPLIT.index(c) - PARTS] + 1)
                act.copy(w_hi[:, parts_of(c)], ring[:, c % RING]).then_inc(hi_done, 1)

            def natural_out(m, h, done):
                act.wait_ge(chunk_done, ORDER.index((m, 2 * h + 1)) + 1)
                act.activation(cut(nat, h), nat_bank[m, h][0:N, :], ACT.Copy, scale=rstd_n[:, 0:1]).then_inc(done, 1)

            def early_split_hi(c):
                landed(act, c)
                act.copy(w_hi[:, parts_of(c), 0:PER], ring[:, c % RING, 0:PER]).then_inc(early_hi, 1)
                act.copy(w_hi[:, parts_of(c), PER:], ring[:, c % RING, PER:]).then_inc(hi_done, 1)

            early_split_hi(4)
            early_split_hi(6)
            early_split_hi(7)
            act.wait_ge(rstd_n_ready, 1)
            natural_out(WK, 0, k_nat)
            act.wait_ge(small_landed, 32)
            act.activation(tw[:, 1, :], tw[:, 0, :], ACT.Abs).then_inc(act_step, 1)
            act.wait_ge(act_step, 1)
            act.activation(tw[:, 2, :], tw[:, 1, :], ACT.Exp, scale=-1.0).then_inc(act_step, 1)
            act.wait_ge(act_step, 2)
            act.activation(tw[:, 3, :], tw[:, 2, :], ACT.Ln, bias=1.0).then_inc(tw_ready, 1)
            early_split_hi(9)
            early_split_hi(10)
            natural_out(WK, 1, k_nat)

            def softmax_exp(g):
                act.wait_ge(prob_ready, g + 1)
                for i in range(4):
                    last = act.activation(prob[0:N, g, i], prob[0:N, g, i], ACT.Exp, bias=smax[:, g, i:i + 1],
                                          accum_out=ssum[:, g, i:i + 1])
                last.then_inc(exped, 1)

            def gelu(i):
                act.wait_ge(hid_ready, i + 1)
                act.activation(cut(hid, i), cut(hid, i), ACT.Gelu).then_inc(gelu_done, 1)
                act.wait_ge(gelu_done, i + 1)
                act.wait_ge(gate_ready, 1)
                for e in range(4 * i, 4 * i + 4):
                    units = hid[:, P * e:P * (e + 1)]
                    last = act.activation(units, units, ACT.Copy, scale=gate[:, e:e + 1])
                last.then_inc(weighed, 1)

            def hidden_hi(i):
                act.wait_ge(hidT_done, i + 1)
                act.copy(quad(g_hi, i), quad_psum(aux[i])).then_inc(hid_hi, 1)

            def probT_copy(g):
                act.wait_ge(probT_done, g + 1)
                act.copy(probT[0:N, g], aux[g][0:N, 0:4 * N].rearrange("p (h n) -> p h n", h=4)).then_inc(probT_out, 1)

            def v2n_copy(i):
                act.wait_ge(chunk_done, ORDER.index((WIV, 2 * i + 1)) + 1)
                act.copy(v2n[:, 8 * i:8 * i + 8], nat_bank[WIV, i][0:N, :].rearrange("p (h d) -> p h d", h=8))\
                    .then_inc(v2n_out, 1)

            def attention_hi(i):
                act.wait_ge(ao_ready, i + 1)
                act.copy(quad(a_hi, i), quad(ao, i)).then_inc(ao_hi, 1)

            def value_hi(i):
                act.wait_ge(v_ready, i + 1)
                act.copy(quad(a_hi, i), quad(v, i)).then_inc(v_hi, 1)

            early_split_hi(12)
            act.wait_ge(kT_done, 2)
            natural_out(WV, 0, v_nat)
            split_hi(15)
            value_hi(0)
            softmax_exp(0)
            softmax_exp(1)
            split_hi(18)
            act.wait_ge(cells_done, 1)
            act.dma_start(x1[:, :], x).then_inc(xn_landed, 16)
            act.dma_start(hid[:, :], bo.to_broadcast([N, D])).then_inc(xn_landed, 16)
            act.dma_start(b1_sb[:, :], b1.to_broadcast([N, D])).then_inc(small_landed, 16)
            split_hi(20)
            split_hi(21)
            natural_out(WV, 1, v_nat)
            split_hi(22)
            value_hi(1)
            split_hi(23)
            probT_copy(0)
            probT_copy(1)
            softmax_exp(2)
            v2n_copy(0)
            softmax_exp(3)
            split_hi(24)
            attention_hi(0)
            split_hi(25)
            probT_copy(2)
            probT_copy(3)
            split_hi(26)
            v2n_copy(1)
            act.dma_start(b2_sb, b2).then_inc(b2_landed, 16)
            split_hi(27)
            attention_hi(1)
            for c in range(28, 31):
                split_hi(c)
            for i in range(4):
                act.wait_ge(xnT_done, i + 1)
                act.copy(pair_of(a_hi, i), pair_psum(aux[i])).then_inc(xn_hi, 1)
            for i in range(4):
                act.wait_ge(xn_lo, i + 1)
                act.copy(pair_of(xnT, i), pair_psum(aux[i])).then_inc(xnT_out, 1)
            for i in range(2):
                act.activation(x1_sq[i], cut(hid, i), ACT.Square, scale=1.0 / D ** 0.5, accum_out=x1_var[:, i:i + 1])\
                    .then_inc(x1_squared, 1)
            split_hi(31)
            split_hi(32)
            act.wait_ge(logits_ready, 1)
            act.activation(gate[:, :], logit[:, :], ACT.Exp, bias=ntop[:, :]).then_inc(gate_exped, 1)
            act.activation(ntop[:, :], ntop[:, :], ACT.Gelu)
            split_hi(33)
            act.wait_ge(gateT_done, 1)
            act.copy(gateT[:, :], aux[3][0:EXPERTS, 0:N]).then_inc(gateT_out, 1)
            gelu(0)
            hidden_hi(0)
            gelu(1)
            early_split_hi(34)
            hidden_hi(1)
            early_split_hi(35)

        @block.vector
        def _(dve):
            steps = [0]

            def then(ins):
                steps[0] += 1
                ins.then_inc(step, 1)
                dve.wait_ge(step, steps[0])

            def pair(c):
                return acc_of(c)[:, 0:PER * N].rearrange("p (t n) -> p t n", t=PER)

            def biases(m, p):
                return bias[:, m, PER * p:PER * (p + 1)].unsqueeze(2).to_broadcast([P, PER, N])

            rstd_pair = rstd[:, :].unsqueeze(1).to_broadcast([P, PER, N])

            dve.wait_ge(x_landed, 16)
            dve.tensor_reduce(part[:, 0], x_sb[:, :, :].rearrange("p t n -> p n t"), axis=AX_X, op=ALU.add)\
                .then_inc(part_ready, 1)
            dve.wait_ge(mean_done, 1)
            for i in range(2):
                dve.tensor_tensor(quad(xc, i), quad(x_sb, i), stat[:, 0:N].unsqueeze(1).to_broadcast([P, KG, N]),
                                  ALU.subtract).then_inc(centered, 1)
            dve.wait_ge(squared, 1)
            dve.tensor_reduce(part[:, 1], sq[:, :, :].rearrange("p t n -> p n t"), axis=AX_X, op=ALU.add)\
                .then_inc(sq_ready, 1)
            dve.wait_ge(rows_landed, 16)
            dve.tensor_copy(erow_b, erow).then_inc(rows_ready, 1)
            dve.wait_ge(edges_landed, 16)
            then(dve.tensor_copy(ecol_f[:, :, :], ecol[:, :, :]))
            then(dve.tensor_scalar(code[:, :], ecol_f[:, 2, :], 0.0, float(TYPES), ALU.is_equal, ALU.mult))
            then(dve.tensor_tensor(code[:, :], code[:, :], ecol_f[:, 2, :], ALU.add))
            dve.wait_ge(const_done, 8)
            dve.tensor_tensor(code[:, :], code[:, :], weight_of_col[:, :], ALU.mult).then_inc(codes_ready, 1)
            then(dve.scalar_tensor_tensor(key_col[:, :], ecol_f[:, 0, :], float(N), ecol_f[:, 1, :],
                                          ALU.mult, ALU.add))
            dve.wait_ge(var_done, 1)
            dve.tensor_scalar(rscr_n[:, 0:1], stat[0:N, 128:129], EPS, None, ALU.add).then_inc(var_out, 1)
            dve.wait_ge(rstd_n_ready, 1)
            dve.tensor_scalar(rdiag[:, :], ident[0:N, 0:N], rstd_n[:, 0:1], None, ALU.mult).then_inc(rdiag_ready, 1)
            dve.wait_ge(rstd_done, 1)
            then(dve.tensor_copy(rstd[:, :], stat[:, 256:256 + N]))
            dve.wait_ge(cols_landed, 16)

            def evacuate(c):
                m, p = ORDER[c]
                dve.wait_ge(chunk_done, c + 1)
                if m == WQ:
                    then(dve.tensor_tensor(pair_of(q, p), pair(c), rstd_pair, ALU.mult))
                    dve.tensor_tensor(pair_of(q, p), pair_of(q, p), biases(0, p), ALU.add).then_inc(evac, 1)
                else:
                    to = {WIQ: q2, WIK: k2}[m]
                    b = {WIQ: 2, WIK: 3}[m]
                    dve.tensor_tensor(pair_of(to, p), pair(c), biases(b, p), ALU.add).then_inc(evac, 1)

            def count_later():
                dve.wait_ge(keys_out, 3)
                for c in range(EC):
                    last = dve.scalar_tensor_tensor(same[:, P * c:P * (c + 1)], keys[:, P * c:P * (c + 1)],
                                                    key_col[:, c:c + 1], later[:, :], ALU.is_equal, ALU.mult,
                                                    accum_out=dup[:, 0, c:c + 1])
                then(last)

            def one_hot_sources():
                then(dve.scalar_tensor_tensor(dup[:, 1], dup[:, 0], float(P), ecol_f[:, 0, :], ALU.mult, ALU.add))
                dve.tensor_tensor(src_hot[:, :, :], iota_f[:, :].unsqueeze(1).to_broadcast([P, EC, N]),
                                  dup[:, 1, :].unsqueeze(2).to_broadcast([P, EC, N]), ALU.is_equal)\
                    .then_inc(src_ready, 1)

            def build_mask():
                dve.wait_ge(tw_ready, 1)
                then(dve.scalar_tensor_tensor(tw[:, 1, :], tw[:, 0, :], 0.0, tw[:, 3, :], ALU.max, ALU.add))
                dve.wait_ge(cells_done, 1)
                then(dve.scalar_tensor_tensor(cell[:, :], ident[0:N, 0:N], 2.0 * TYPES / DIGIT, aux[3][0:N, 0:N],
                                              ALU.mult, ALU.add))
                then(dve.tensor_scalar(mask[:, :], cell[:, :], 0.0, ABSENT, ALU.is_equal, ALU.mult))
                then(dve.tensor_scalar(digit_i[:, :], cell[:, :].bitcast(I32), 22, 7,
                                       ALU.logical_shift_right, ALU.bitwise_and))
                then(dve.tensor_copy(cell[:, :], digit_i[:, :]))
                for t in range(TYPES):
                    then(dve.tensor_scalar(cell_t[:, :], cell[:, :], float((0, 2, 3, 4)[t]), tw[:, 1, t:t + 1],
                                           ALU.is_equal, ALU.mult))
                    then(dve.tensor_tensor(mask[:, :], mask[:, :], cell_t[:, :], ALU.add))

            def scores(g):
                dve.wait_ge(scores_done, g // 2 + 1)
                s = prob[0:N, g]
                dve.scalar_tensor_tensor(s, aux[g][0:N, 0:4 * N].rearrange("p (h n) -> p h n", h=4), SCALE,
                                         mask[:, :].unsqueeze(1).to_broadcast([N, 4, N]), ALU.mult, ALU.add)\
                    .then_inc(scores_out, 1)
                dve.wait_ge(scores_out, g + 1)
                then(dve.tensor_reduce(smax[:, g], s, axis=AX_X, op=ALU.max))
                dve.tensor_scalar(smax[:, g], smax[:, g], -1.0, None, ALU.mult).then_inc(prob_ready, 1)

            def normalise(g):
                dve.wait_ge(exped, g + 1)
                s = prob[0:N, g]
                then(dve.reciprocal(sinv[:, g], ssum[:, g]))
                dve.tensor_tensor(s, s, sinv[:, g].unsqueeze(2).to_broadcast([N, 4, N]), ALU.mult)\
                    .then_inc(prob_normed, 1)

            def split_lo(c):
                dve.wait_ge(hi_done, SPLIT.index(c) + 1)
                dve.tensor_tensor(w_lo[:, parts_of(c)], ring[:, c % RING], w_hi[:, parts_of(c)].bitcast(F32),
                                  ALU.subtract).then_inc(lo_done, 1)

            def early_split_lo(c):
                for engine_sem, made, part in ((early_hi, early_lo, slice(0, PER)), (hi_done, lo_done, slice(PER, KG))):
                    dve.wait_ge(engine_sem, (EARLY if made is early_lo else SPLIT).index(c) + 1)
                    dve.tensor_tensor(w_lo[:, parts_of(c), part], ring[:, c % RING, part],
                                      w_hi[:, parts_of(c), part].bitcast(F32), ALU.subtract).then_inc(made, 1)

            def key_tiles(i):
                dve.wait_ge(kT_done, i + 1)
                dve.tensor_tensor(quad(k, i), quad_psum(aux[i]),
                                  bias[:, 1, KG * i:KG * (i + 1)].unsqueeze(2).to_broadcast([P, KG, N]), ALU.add)\
                    .then_inc(k_ready, 1)

            def value_tiles(i):
                dve.wait_ge(vT_done, i + 1)
                dve.tensor_tensor(quad(v, i), quad_psum((aux[0], stat)[i]),
                                  bias[:, 4, KG * i:KG * (i + 1)].unsqueeze(2).to_broadcast([P, KG, N]), ALU.add)\
                    .then_inc(v_ready, 1)

            def value_lo(i):
                dve.wait_ge(v_ready, i + 1)
                dve.wait_ge(v_hi, i + 1)
                dve.tensor_tensor(quad(a_lo, i), quad(v, i), quad(a_hi, i).bitcast(F32), ALU.subtract).then_inc(v_lo, 1)

            evacuate(0)
            dve.wait_ge(xc_hi, 1)
            dve.tensor_tensor(g_lo[:, :, :], xc[:, :, :], g_hi[:, :, :].bitcast(F32), ALU.subtract).then_inc(xc_lo, 1)
            evacuate(1)
            evacuate(2)
            early_split_lo(4)
            evacuate(3)
            early_split_lo(6)
            evacuate(5)
            early_split_lo(7)
            count_later()
            early_split_lo(9)
            key_tiles(0)
            evacuate(8)
            early_split_lo(10)
            key_tiles(1)
            one_hot_sources()
            early_split_lo(12)
            build_mask()
            evacuate(11)
            split_lo(15)
            evacuate(13)
            value_tiles(0)
            value_lo(0)
            evacuate(14)

            def attention_sum(i):
                dve.wait_ge(heads_done, i + 1)
                dve.tensor_tensor(quad(ao, i), quad_psum(aux[i]),
                                  bias[:, 5, KG * i:KG * (i + 1)].unsqueeze(2).to_broadcast([P, KG, N]), ALU.add)\
                    .then_inc(ao_ready, 1)

            def attention_lo(i):
                dve.wait_ge(ao_ready, i + 1)
                dve.wait_ge(ao_hi, i + 1)
                dve.tensor_tensor(quad(a_lo, i), quad(ao, i), quad(a_hi, i).bitcast(F32), ALU.subtract)\
                    .then_inc(ao_lo, 1)

            def first_residual(i):
                dve.wait_ge(chunk_done, ORDER.index((WO, 2 + i)) + 1)
                dve.scalar_tensor_tensor(cut(x1, i), nat_bank[WO, i][0:N, :], 1.0, cut(x1, i), ALU.mult, ALU.add,
                                         accum_out=x1_sum[:, i:i + 1]).then_inc(x1_ready, 1)

            scores(0)
            scores(1)
            normalise(0)
            normalise(1)
            split_lo(18)
            evacuate(16)
            split_lo(20)
            evacuate(17)
            split_lo(21)
            split_lo(22)
            evacuate(19)
            value_tiles(1)
            value_lo(1)
            scores(2)
            scores(3)
            normalise(2)
            split_lo(23)
            normalise(3)
            attention_sum(0)
            split_lo(24)
            attention_lo(0)
            split_lo(25)
            split_lo(26)
            attention_sum(1)
            attention_lo(1)
            split_lo(27)
            split_lo(28)
            dve.wait_ge(xb_ready, 1)
            first_residual(0)
            first_residual(1)
            dve.wait_ge(x1_ready, 2)
            then(dve.tensor_scalar(x1_mean[:, :], x1_sum[:, 0:1], x1_sum[:, 1:2], 1.0 / D, ALU.add, ALU.mult))
            for i in range(4):
                dve.tensor_scalar(hid[:, PER * P * i:PER * P * (i + 1)], x1[:, PER * P * i:PER * P * (i + 1)],
                                  x1_mean[:, :], None, ALU.subtract).then_inc(x1_centered, 1)
            for i in range(4):
                dve.wait_ge(xn_hi, i + 1)
                dve.tensor_tensor(pair_of(a_lo, i), pair_psum(aux[i]), pair_of(a_hi, i).bitcast(F32), ALU.subtract)\
                    .then_inc(xn_lo, 1)
            split_lo(29)
            dve.wait_ge(x1_squared, 2)
            dve.tensor_scalar(rscr_n[:, 1:2], x1_var[:, 0:1], x1_var[:, 1:2], EPS, ALU.add, ALU.add).then_inc(var_out, 1)
            split_lo(30)
            dve.wait_ge(logits_done, 1)
            dve.wait_ge(small_landed, 48)
            dve.wait_ge(rstd_n_ready, 2)
            then(dve.scalar_tensor_tensor(logit[:, :], aux[2][0:N, 0:EXPERTS], rstd_n[:, 1:2], br_sb[:, :],
                                          ALU.mult, ALU.add))
            then(dve.max(top[:, :], logit[:, :]))
            dve.tensor_scalar(ntop[:, :], top[:, 0:1], -1.0, None, ALU.mult).then_inc(logits_ready, 1)
            dve.wait_ge(gate_exped, 1)
            then(dve.scalar_tensor_tensor(gate[:, :], logit[:, :], top[:, 1:2], gate[:, :], ALU.is_ge, ALU.mult))
            then(dve.tensor_reduce(gsum[:, 0:1], gate[:, :], axis=AX_X, op=ALU.add))
            then(dve.reciprocal(gsum[:, 1:2], gsum[:, 0:1]))
            dve.tensor_scalar(gate[:, :], gate[:, :], gsum[:, 1:2], None, ALU.mult).then_inc(gate_ready, 1)

            def hidden(i):
                dve.wait_ge(chunk_done, ORDER.index((W1, 2 * i + 1)) + 1)
                dve.scalar_tensor_tensor(cut(hid, i), nat_bank[W1, i][0:N, :], rstd_n[:, 1:2], cut(b1_sb, i),
                                         ALU.mult, ALU.add).then_inc(hid_ready, 1)

            def hidden_lo(i):
                dve.wait_ge(hid_hi, i + 1)
                dve.tensor_tensor(quad(g_lo, i), quad_psum(aux[i]), quad(g_hi, i).bitcast(F32), ALU.subtract)\
                    .then_inc(hid_lo, 1)

            split_lo(31)
            hidden(0)
            split_lo(32)
            hidden(1)
            hidden_lo(0)
            split_lo(33)
            early_split_lo(34)
            hidden_lo(1)
            early_split_lo(35)
            for i, (lo, hi) in enumerate(OUT_PARTS):
                dve.wait_ge(chunk_done, CHUNKS + i)
                to = (nat_bank[W2, 0], stat, acc[0])[i]
                dve.tensor_tensor(res[:, lo:hi], to[0:N, lo % HALF:lo % HALF + hi - lo], x1[:, lo:hi], ALU.add)\
                    .then_inc(res_ready, 1)

        @block.tensor
        def _(pe):
            def stationary_chunk(c, rhs, ready):
                landed(pe, c)
                if WHOLE.index(c) >= ACC:
                    pe.wait_ge(evac, WHOLE.index(c) - ACC + 1)
                w = ring[:, c % RING].rearrange("p a b -> p (a b)").rearrange("p (t k j) -> p t k j", t=PER, k=KT)
                for t in range(PER):
                    for kt in range(KT):
                        if t == 0:
                            ready(kt)
                        last = nc.tensor.matmul(acc_of(c)[:, N * t:N * (t + 1)], w[:, t, kt],
                                                rhs[:, kt], start=(kt == 0), stop=(kt == KT - 1))
                last.then_inc(chunk_done, 1)

            def nothing(kt):
                pass

            def split_chunk(c, hi, lo, bank=None, first=0, end=HALF, made=None):
                m, kg, h = chunk_of(c)
                if c in EARLY:
                    pe.wait_ge(early_lo, EARLY.index(c) + 1)
                else:
                    pe.wait_ge(lo_done, SPLIT.index(c) + 1)
                out_ = (bank or nat_bank[m, h])[0:N, first:end]
                for i in range(KG):
                    kt = KG * kg + i
                    if c in EARLY and i == PER:
                        pe.wait_ge(lo_done, SPLIT.index(c) + 1)
                    if made is not None and kt % PER == 0:
                        pe.wait_ge(made, kt // PER + 1)
                    nc.tensor.matmul(out_, hi[:, kt], w_hi[:, parts_of(c), i, first:end],
                                     start=(m != W2 and kg == 0 and i == 0), stop=False)
                    nc.tensor.matmul(out_, hi[:, kt], w_lo[:, parts_of(c), i, first:end], start=False, stop=False)
                    last = nc.tensor.matmul(out_, lo[:, kt], w_hi[:, parts_of(c), i, first:end], start=False,
                                            stop=(kg == 1 and i == KG - 1))
                last.then_inc(chunk_done, 1)

            def keep_warm(n):
                idle = mean_w[:, :].bitcast(BF16)
                for i in range(n):
                    nc.tensor.matmul(acc[1][:, 0:2 * P], idle[:, 0:P], idle[:, :], start=True, stop=True)

            pe.wait_ge(warm_ready, 1)
            for i in range(WARM):
                nc.tensor.matmul(acc[ACC - 1][:, :], warm[:, 0:P], warm[:, :], start=True, stop=True)
            pe.wait_ge(const_done, 8)
            pe.wait_ge(part_ready, 1)
            nc.tensor.matmul(stat[:, 0:N], mean_w[:, :], part[:, 0], start=True, stop=True).then_inc(mean_done, 1)
            for i in range(WARM_2):
                nc.tensor.matmul(acc[ACC - 1][:, :], warm[:, 0:P], warm[:, :], start=True, stop=True)

            def ready_centered(kt):
                if kt % 4 == 0:
                    pe.wait_ge(centered, kt // 4 + 1)

            stationary_chunk(0, xc, ready_centered)
            pe.wait_ge(sq_ready, 1)
            nc.tensor.matmul(stat[0:N, 128:129], part[:, 1], mean_w[:, 0:1], start=True, stop=True).then_inc(var_done, 1)
            stationary_chunk(1, xc, nothing)
            pe.wait_ge(rdiag_ready, 1)
            nc.tensor.matmul(stat[:, 256:256 + N], ones[:, :], rdiag[:, :], start=True, stop=True).then_inc(rstd_done, 1)
            pe.wait_ge(rows_ready, 1)
            for i in range(3):
                nc.tensor.matmul(aux[i][:, :], key_w[:, :], erow_b[:, 512 * i:512 * (i + 1)],
                                 start=True, stop=True).then_inc(keys_done, 1)

            def natural_transposed(to, rows, i, tiles=KG):
                for t in range(tiles):
                    kt = tiles * i + t
                    last = nc.tensor.transpose(to[:, N * t:N * (t + 1)], rows[:, P * kt:P * (kt + 1)], ident[0:N, 0:N])
                return last

            stationary_chunk(2, xc, nothing)
            stationary_chunk(3, xc, nothing)
            pe.wait_ge(xc_lo, 1)
            split_chunk(4, g_hi, g_lo)

            def ready_q(kt):
                if kt == 0:
                    pe.wait_ge(evac, 4)

            def ready_k(kt):
                if kt % KG == 0:
                    pe.wait_ge(k_ready, kt // KG + 1)

            stationary_chunk(5, q, ready_q)
            split_chunk(6, g_hi, g_lo)
            split_chunk(7, g_hi, g_lo)
            pe.wait_ge(k_nat, 1)
            pe.wait_ge(keys_out, 3)
            natural_transposed(aux[0], nat, 0).then_inc(kT_done, 1)
            stationary_chunk(8, q, nothing)
            split_chunk(9, g_hi, g_lo)
            split_chunk(10, g_hi, g_lo)
            pe.wait_ge(k_nat, 2)
            natural_transposed(aux[1], nat, 1).then_inc(kT_done, 1)
            stationary_chunk(11, k, ready_k)
            pe.wait_ge(src_ready, 1)
            pe.wait_ge(dst_ready, 1)
            for c in range(EC):
                last = nc.tensor.matmul(aux[3][0:N, 0:N], src_hot[:, c], dst_hot[:, c],
                                        start=(c == 0), stop=(c == EC - 1))
            last.then_inc(cells_done, 1)
            split_chunk(12, g_hi, g_lo)
            stationary_chunk(13, k, nothing)
            pe.wait_ge(v_nat, 1)
            natural_transposed(aux[0], nat, 0).then_inc(vT_done, 1)
            stationary_chunk(14, q, nothing)

            def all_scores(half):
                for h in range(8 * half, 8 * half + 8):
                    g, i, s = 2 * (h // 8) + h % 2, (h % 8) // 2, HD * (h % 2)
                    last = nc.tensor.matmul(aux[g][0:N, N * i:N * (i + 1)], q2[s:s + HD, h // 2], k2[s:s + HD, h // 2],
                                            start=True, stop=True)
                last.then_inc(scores_done, 1)

            pe.wait_ge(evac, WHOLE.index(13) + 1)
            pe.wait_ge(v_ready, 1)
            all_scores(0)
            split_chunk(15, g_hi, g_lo)
            stationary_chunk(16, q, nothing)
            stationary_chunk(17, k, nothing)
            split_chunk(18, g_hi, g_lo)
            stationary_chunk(19, k, nothing)
            pe.wait_ge(v_nat, 2)
            natural_transposed(stat, nat, 1).then_inc(vT_done, 1)
            pe.wait_ge(v_lo, 1)
            split_chunk(20, a_hi, a_lo)
            pe.wait_ge(evac, len(WHOLE))
            all_scores(1)

            def probs_transposed(g):
                pe.wait_ge(prob_normed, g + 1)
                for i in range(4):
                    last = nc.tensor.transpose(aux[g][0:N, N * i:N * (i + 1)], prob[0:N, g, i], ident[0:N, 0:N])
                last.then_inc(probT_done, 1)

            def attend(i):
                pe.wait_ge(v2n_out, i + 1)
                pe.wait_ge(probT_out, 2 * i + 2)
                for t in range(4):
                    for s in range(2):
                        h = 2 * (4 * i + t) + s
                        g, j = 2 * (h // 8) + h % 2, (h % 8) // 2
                        last = nc.tensor.matmul(aux[i][HD * s:HD * (s + 1), N * t:N * (t + 1)], v2n[:, h],
                                                probT[0:N, g, j], start=True, stop=True)
                last.then_inc(heads_done, 1)

            probs_transposed(0)
            probs_transposed(1)
            pe.wait_ge(v_lo, 2)
            split_chunk(21, a_hi, a_lo)
            split_chunk(22, a_hi, a_lo)
            attend(0)
            split_chunk(23, a_hi, a_lo)
            probs_transposed(2)
            probs_transposed(3)
            pe.wait_ge(ao_lo, 1)
            split_chunk(24, a_hi, a_lo)
            attend(1)
            split_chunk(25, a_hi, a_lo)
            pe.wait_ge(ao_lo, 2)
            split_chunk(26, a_hi, a_lo)
            split_chunk(27, a_hi, a_lo)
            keep_warm(WARM_LN)
            for i in range(4):
                pe.wait_ge(x1_centered, i + 1)
                natural_transposed(aux[i], hid, i, PER).then_inc(xnT_done, 1)
            keep_warm(WARM_XN)
            split_chunk(28, a_hi, a_lo, made=xn_lo)
            pe.wait_ge(xn_lo, 4)
            pe.wait_ge(xnT_out, 4)
            for kt in range(KT):
                last = nc.tensor.matmul(aux[2][0:N, 0:EXPERTS], xnT[:, kt], wr[:, kt], start=(kt == 0), stop=(kt == KT - 1))
            last.then_inc(logits_done, 1)
            split_chunk(29, a_hi, a_lo)
            split_chunk(30, a_hi, a_lo)
            pe.wait_ge(gate_ready, 1)
            nc.tensor.transpose(aux[3][0:EXPERTS, 0:N], gate[:, :], ident[0:N, 0:N]).then_inc(gateT_done, 1)
            split_chunk(31, a_hi, a_lo)
            pe.wait_ge(weighed, 1)
            natural_transposed(aux[0], hid, 0).then_inc(hidT_done, 1)
            pe.wait_ge(gateT_out, 1)
            pe.wait_ge(b2_landed, 16)
            nc.tensor.matmul(nat_bank[W2, 0][0:N, :], gateT[:, :], cut(b2_sb, 0), start=True, stop=False)
            for to, first, end in W2_QUARTERS:
                nc.tensor.matmul(to[0:N, first:end], gateT[:, :], b2_sb[:, HALF + first:HALF + end], start=True, stop=False)
            pe.wait_ge(hid_lo, 1)
            split_chunk(32, g_hi, g_lo)
            split_chunk(33, g_hi, g_lo, *W2_QUARTERS[0])
            pe.wait_ge(weighed, 2)
            natural_transposed(aux[1], hid, 1).then_inc(hidT_done, 1)
            split_chunk(33, g_hi, g_lo, *W2_QUARTERS[1])
            pe.wait_ge(hid_lo, 2)
            split_chunk(34, g_hi, g_lo)
            for quarter in W2_QUARTERS:
                split_chunk(35, g_hi, g_lo, *quarter)


def kernel(x, src, dst, edge_type_5, L0_gnn_edge_type_weights, L0_gnn_wq, L0_gnn_bq, L0_gnn_wk, L0_gnn_bk, L0_gnn_wv,
           L0_gnn_bv, L0_gnn_wiq, L0_gnn_biq, L0_gnn_wik, L0_gnn_bik, L0_gnn_wiv, L0_gnn_biv, L0_gnn_wo, L0_gnn_bo,
           L0_ffn_W1, L0_ffn_b1, L0_ffn_W2, L0_ffn_b2, L0_ffn_Wr, L0_ffn_br):
    import numpy as np
    import concourse.bacc as bacc
    from concourse.bass_utils import run_bass_kernel_spmd

    a = np.asarray

    def stationary(w_out_in):
        return a(w_out_in).reshape(CPM, PER, P, KT, P).transpose(0, 4, 1, 3, 2).reshape(CPM, P, KG, HALF)

    def moving(w_in_out, half_first=False):
        order = (3, 0, 2, 1, 4) if half_first else (0, 3, 2, 1, 4)
        return w_in_out.reshape(2, KG, P, 2, HALF).transpose(order).reshape(CPM, P, KG, HALF)

    mats = [stationary(L0_gnn_wq), moving(a(L0_gnn_wk).T, half_first=True), stationary(L0_gnn_wiq),
            stationary(L0_gnn_wik), moving(a(L0_gnn_wv).T, half_first=True),
            moving(a(L0_gnn_wiv).T, half_first=True), moving(a(L0_gnn_wo).T),
            moving(a(L0_ffn_W1).transpose(1, 0, 2), half_first=True), moving(a(L0_ffn_W2))]
    biases = np.stack([a(b).reshape(8, P) for b in (L0_gnn_bq, L0_gnn_bk, L0_gnn_biq, L0_gnn_bik, L0_gnn_bv,
                                                    L0_gnn_biv)])
    router = a(L0_ffn_Wr).reshape(KT, P, EXPERTS)
    edges = np.stack([a(e) for e in (src, dst, edge_type_5)])
    arrays = {
        "xT": np.ascontiguousarray(a(x).T.reshape(KT, P, N).transpose(1, 0, 2)),
        "x": a(x),
        "weights": np.stack([mats[m][i] for m, i in ORDER]),
        "cols": np.ascontiguousarray(np.concatenate([biases.transpose(2, 0, 1), router.transpose(1, 0, 2)], axis=1)),
        "edge_cols": np.ascontiguousarray(edges.reshape(3, EC, P).transpose(2, 0, 1)),
        "edge_rows": np.ascontiguousarray(edges[0:2]),
        "type_weights": a(L0_gnn_edge_type_weights).reshape(1, TYPES),
        "bo": a(L0_gnn_bo).reshape(1, D),
        "b1": a(L0_ffn_b1).reshape(1, D),
        "br": a(L0_ffn_br).reshape(1, EXPERTS),
        "b2": a(L0_ffn_b2),
    }
    nc = bacc.Bacc("TRN2", target_bir_lowering=False, num_devices=1)
    args = [nc.dram_tensor(n, v.shape, mybir.dt.from_np(v.dtype), kind="ExternalInput").ap() for n, v in arrays.items()]
    args.append(nc.dram_tensor("out", (N, D), F32, kind="ExternalOutput").ap())
    gnn_ffn_kernel(nc, *args)
    r = run_bass_kernel_spmd(nc, [arrays], core_ids=[0])
    return r.results[0]["out"]
```
